# Optimizing a Trainium2 kernel written in Bass

```python
import numpy as np
import jax
import jax.numpy as jnp

def _softmax(x, axis=-1):
    return jax.nn.softmax(x, axis=axis)

def _gelu(x):
    return jax.nn.gelu(x, approximate=True)

def _silu(x):
    return jax.nn.silu(x)

def _sigmoid(x):
    return jax.nn.sigmoid(x)

def _layernorm(x, axis=-1, eps=1e-05):
    m = jnp.mean(x, axis=axis, keepdims=True)
    v = jnp.var(x, axis=axis, keepdims=True)
    return (x - m) / jnp.sqrt(v + eps)

def _scatter_add(tgt, idx, src, axis=0):
    return tgt.at[idx].add(src)

def _segment_sum(src, seg, n):
    return jax.ops.segment_sum(src, seg, n)
kernel_name = 'mk_decoder_preln_d1_seqx_r4_ea51df'

def setup_inputs(seed: int=0):
    np.random.seed(seed)
    _w = jnp.asarray

    def _rec_inputs():
        import jax
        import jax.numpy as jnp
        _rk = jax.random.key(seed)
        x = 7.22e-05 + 1 * jax.random.normal(jax.random.fold_in(_rk, 1), (4, 1024, 256), jnp.float32)
        _lenS = 1024 - jax.random.randint(jax.random.fold_in(_rk, 7), (4,), 0, max(1, 1024 // 4) + 1, jnp.int32)
        _lenS2 = 64 - jax.random.randint(jax.random.fold_in(_rk, 8), (4,), 0, max(1, 64 // 4) + 1, jnp.int32)
        _ctx_1024P = jax.random.normal(jax.random.fold_in(_rk, 11), (4, 16, 256), jnp.float32)
        _ctx_1024c = jax.random.dirichlet(jax.random.fold_in(_rk, 511), 0.3 * jnp.ones((16,), jnp.float32), (4, 64))
        _ctx_1024t = jnp.einsum('bsk,bkd->bsd', _ctx_1024c, _ctx_1024P)
        _ctx_1024t = _ctx_1024t * jax.lax.rsqrt(jnp.mean(jnp.square(_ctx_1024t)) + 1e-12) * 0.953939
        ctx_1024 = 4.13588e-05 + 0.999923 * (_ctx_1024t + 0.3 * jax.random.normal(jax.random.fold_in(_rk, 611), (4, 64, 256), jnp.float32))
        return (x, ctx_1024)
    x, ctx_1024 = _rec_inputs()

    def _L0_attn_setup():
        import jax, jax.numpy as jnp
        import numpy as np
        from math import sqrt
        EMBED = 256
        HEADS = 16
        key = jax.random.key(seed)
        k1, k2, k3, k4, k5 = jax.random.split(key, 5)
        x = jax.random.normal(k1, (2, 512, EMBED), dtype=jnp.float32)
        s = 1.0 / sqrt(EMBED)
        W_qkv = jax.random.normal(k2, (EMBED, 3 * EMBED), dtype=jnp.float32) * s
        b_qkv = jax.random.normal(k3, (3 * EMBED,), dtype=jnp.float32) * 0.01
        W_out = jax.random.normal(k4, (EMBED, EMBED), dtype=jnp.float32) * s
        b_out = jax.random.normal(k5, (EMBED,), dtype=jnp.float32) * 0.01
        return {'x': x, 'W_qkv': W_qkv, 'b_qkv': b_qkv, 'W_out': W_out, 'b_out': b_out}
    _L0_attn_all = _L0_attn_setup()
    _L0_attn_in = {k: v for k, v in _L0_attn_all.items() if k in ('W_qkv', 'b_qkv', 'W_out', 'b_out')}
    del _L0_attn_all

    def _L0_xattn_setup():
        import jax, jax.numpy as jnp
        import numpy as np
        D_MODEL = 256
        NUM_HEADS = 16
        D_K = D_MODEL // NUM_HEADS

        def _split_heads(x):
            B, S, _ = x.shape
            return x.reshape(B, S, NUM_HEADS, D_K).transpose(0, 2, 1, 3)
        key = jax.random.key(seed)
        ks = jax.random.split(key, 11)
        B, S = (4, 512)
        scale = 1.0 / np.sqrt(D_MODEL)
        inp = {'query': jax.random.normal(ks[0], (B, S, D_MODEL), jnp.float32), 'key': jax.random.normal(ks[1], (B, S, D_MODEL), jnp.float32), 'value': jax.random.normal(ks[2], (B, S, D_MODEL), jnp.float32), 'Wq': jax.random.normal(ks[3], (D_MODEL, D_MODEL), jnp.float32) * scale, 'bq': jnp.zeros((D_MODEL,), jnp.float32), 'Wk': jax.random.normal(ks[4], (D_MODEL, D_MODEL), jnp.float32) * scale, 'bk': jnp.zeros((D_MODEL,), jnp.float32), 'Wv': jax.random.normal(ks[5], (D_MODEL, D_MODEL), jnp.float32) * scale, 'bv': jnp.zeros((D_MODEL,), jnp.float32), 'Wo': jax.random.normal(ks[6], (D_MODEL, D_MODEL), jnp.float32) * scale, 'bo': jnp.zeros((D_MODEL,), jnp.float32)}
        return inp
    _L0_xattn_all = _L0_xattn_setup()
    _L0_xattn_in = {k: v for k, v in _L0_xattn_all.items() if k in ('Wq', 'bq', 'Wk', 'bk', 'Wv', 'bv', 'Wo', 'bo')}
    del _L0_xattn_all

    def _L0_ffn_setup():
        import jax, jax.numpy as jnp
        import numpy as np
        EPS = 1e-06
        LN_EPS = 1e-05

        def _absmean_core(W):
            gamma = jnp.mean(jnp.abs(W)) + EPS
            Ws = W / gamma
            Wq = jnp.sign(Ws) * jnp.minimum(jnp.round(jnp.abs(Ws)), 1.0)
            return (Wq, gamma)

        @jax.custom_vjp
        def absmean(W):
            return _absmean_core(W)[0]

        def _absmean_fwd(W):
            Wq, gamma = _absmean_core(W)
            return (Wq, gamma)

        def _absmean_bwd(gamma, g):
            return (g / gamma,)
        absmean.defvjp(_absmean_fwd, _absmean_bwd)

        def layernorm(x, w, b, eps=LN_EPS):
            mu = jnp.mean(x, axis=-1, keepdims=True)
            var = jnp.mean((x - mu) ** 2, axis=-1, keepdims=True)
            return (x - mu) * jax.lax.rsqrt(var + eps) * w + b
        key = jax.random.key(seed)
        k1, k2, k3 = jax.random.split(key, 3)
        d, h = (256, 1024)
        B, T = (8, 512)
        return {'x': jax.random.normal(k1, (B, T, d), jnp.float32), 'W_fc': jax.random.normal(k2, (h, d), jnp.float32), 'ln_w': jnp.ones((h,), jnp.float32), 'ln_b': jnp.zeros((h,), jnp.float32), 'W_proj': jax.random.normal(k3, (d, h), jnp.float32)}
    _L0_ffn_all = _L0_ffn_setup()
    _L0_ffn_in = {k: v for k, v in _L0_ffn_all.items() if k in ('W_fc', 'ln_w', 'ln_b', 'W_proj')}
    del _L0_ffn_all
    return {'x': x, 'ctx_1024': ctx_1024, 'L0_attn_W_qkv': _L0_attn_in['W_qkv'], 'L0_attn_b_qkv': _L0_attn_in['b_qkv'], 'L0_attn_W_out': _L0_attn_in['W_out'], 'L0_attn_b_out': _L0_attn_in['b_out'], 'L0_xattn_Wq': _L0_xattn_in['Wq'], 'L0_xattn_bq': _L0_xattn_in['bq'], 'L0_xattn_Wk': _L0_xattn_in['Wk'], 'L0_xattn_bk': _L0_xattn_in['bk'], 'L0_xattn_Wv': _L0_xattn_in['Wv'], 'L0_xattn_bv': _L0_xattn_in['bv'], 'L0_xattn_Wo': _L0_xattn_in['Wo'], 'L0_xattn_bo': _L0_xattn_in['bo'], 'L0_ffn_W_fc': _L0_ffn_in['W_fc'], 'L0_ffn_ln_w': _L0_ffn_in['ln_w'], 'L0_ffn_ln_b': _L0_ffn_in['ln_b'], 'L0_ffn_W_proj': _L0_ffn_in['W_proj']}

def reference(x, ctx_1024, L0_attn_W_qkv, L0_attn_b_qkv, L0_attn_W_out, L0_attn_b_out, L0_xattn_Wq, L0_xattn_bq, L0_xattn_Wk, L0_xattn_bk, L0_xattn_Wv, L0_xattn_bv, L0_xattn_Wo, L0_xattn_bo, L0_ffn_W_fc, L0_ffn_ln_w, L0_ffn_ln_b, L0_ffn_W_proj):
    import jax
    import jax.numpy as jnp

    def _L0_attn_ref(x, W_qkv, b_qkv, W_out, b_out):
        import jax, jax.numpy as jnp
        import numpy as np
        from math import sqrt
        EMBED = 256
        HEADS = 16
        B, N, E = x.shape
        H = HEADS
        d = E // H
        qkv = x @ W_qkv + b_qkv
        q, k, v = jnp.split(qkv, 3, axis=2)
        q = q.reshape(B, N, H, d)
        k = k.reshape(B, N, H, d)
        v = v.reshape(B, N, H, d)
        energy = jnp.einsum('bqhe,bkhe->bqhk', q, k)
        attn = jax.nn.softmax(energy, axis=-1) / sqrt(E)
        out = jnp.einsum('bihv,bvhd->bihd', attn, v)
        out = out.reshape(B, N, E)
        return out @ W_out + b_out

    def _L0_xattn_ref(query, key, value, Wq, bq, Wk, bk, Wv, bv, Wo, bo):
        import jax, jax.numpy as jnp
        import numpy as np
        D_MODEL = 256
        NUM_HEADS = 16
        D_K = D_MODEL // NUM_HEADS

        def _split_heads(x):
            B, S, _ = x.shape
            return x.reshape(B, S, NUM_HEADS, D_K).transpose(0, 2, 1, 3)
        q = _split_heads(query @ Wq.T + bq)
        k = _split_heads(key @ Wk.T + bk)
        v = _split_heads(value @ Wv.T + bv)
        scores = jnp.einsum('bhqd,bhkd->bhqk', q, k) / jnp.sqrt(jnp.float32(D_K))
        attn = jax.nn.softmax(scores, axis=-1)
        out = jnp.einsum('bhqk,bhkd->bhqd', attn, v)
        B, H, Sq, dk = out.shape
        out = out.transpose(0, 2, 1, 3).reshape(B, Sq, D_MODEL)
        return out @ Wo.T + bo

    def _L0_ffn_ref(x, W_fc, ln_w, ln_b, W_proj):
        import jax, jax.numpy as jnp
        import numpy as np
        EPS = 1e-06
        LN_EPS = 1e-05

        def _absmean_core(W):
            gamma = jnp.mean(jnp.abs(W)) + EPS
            Ws = W / gamma
            Wq = jnp.sign(Ws) * jnp.minimum(jnp.round(jnp.abs(Ws)), 1.0)
            return (Wq, gamma)

        @jax.custom_vjp
        def absmean(W):
            return _absmean_core(W)[0]

        def _absmean_fwd(W):
            Wq, gamma = _absmean_core(W)
            return (Wq, gamma)

        def _absmean_bwd(gamma, g):
            return (g / gamma,)
        absmean.defvjp(_absmean_fwd, _absmean_bwd)

        def layernorm(x, w, b, eps=LN_EPS):
            mu = jnp.mean(x, axis=-1, keepdims=True)
            var = jnp.mean((x - mu) ** 2, axis=-1, keepdims=True)
            return (x - mu) * jax.lax.rsqrt(var + eps) * w + b
        h = jnp.einsum('btd,hd->bth', x, absmean(W_fc))
        h = jax.nn.gelu(h, approximate=False)
        h = layernorm(h, ln_w, ln_b)
        return jnp.einsum('bth,dh->btd', h, absmean(W_proj))
    x = x + _L0_attn_ref(_layernorm(x, axis=-1), L0_attn_W_qkv, L0_attn_b_qkv, L0_attn_W_out, L0_attn_b_out)
    x = x + _L0_xattn_ref(_layernorm(x, axis=-1), ctx_1024, ctx_1024, L0_xattn_Wq, L0_xattn_bq, L0_xattn_Wk, L0_xattn_bk, L0_xattn_Wv, L0_xattn_bv, L0_xattn_Wo, L0_xattn_bo)
    x = x + _L0_ffn_ref(_layernorm(x, axis=-1), L0_ffn_W_fc, L0_ffn_ln_w, L0_ffn_ln_b, L0_ffn_W_proj)
    return x

_drawn_inputs = setup_inputs


def setup_inputs(seed=0):
    import zlib

    import numpy as np

    out = dict(_drawn_inputs(seed))
    spreads = {'L0_xattn_bq': (0.0, 0.271),
     'L0_xattn_bk': (0.0, 2.0),
     'L0_xattn_bv': (0.0, 0.1),
     'L0_xattn_bo': (0.0, 0.1),
     'L0_ffn_ln_w': (1.0, 0.2),
     'L0_ffn_ln_b': (0.0, 0.1)}
    factors = {'L0_attn_b_qkv': 54.371, 'L0_attn_b_out': 5.957}
    for name, (base, spread) in spreads.items():
        noise = np.random.default_rng([zlib.crc32(name.encode()), seed]).standard_normal(out[name].shape)
        drawn = base * np.exp(spread * noise) if base else spread * noise
        out[name] = jnp.asarray(drawn.astype(out[name].dtype))
    for name, factor in factors.items():
        out[name] = (out[name] * factor).astype(out[name].dtype)
    return out
```

```python
from contextlib import ExitStack

import concourse.bass as bass
from concourse import mybir

F32 = mybir.dt.float32
BF16 = mybir.dt.bfloat16
ALU = mybir.AluOpType
ACT = mybir.ActivationFunctionType
AX = mybir.AxisListType

P = 128
B, S, E = 4, 1024, 256
H, D = 16, 16
CTX = 64
F = 1024
T = B * S
CH = 512
NCH = T // CH
BLK = CH // P
KT = E // P
HG = 4
NG = H // HG
GROUPS = B * NG
KB = S // P
QC = S // CH
MSLOTS = 66
UNITS = QC * KB
MAXT = UNITS * 4
SLOTS_Q = (0, 0, 1, 1, 0, 2)
SLOTS_K = (0, 1, 0, 1, 2, 0)
STACK = len(SLOTS_Q) * D
ROWS = STACK + 3
GROUP_LOADS = 16 * (2 * len(SLOTS_Q) + 1)
HT = F // P
PAIRS = H // 2
LN_EPS = 1e-5
ABS_EPS = 1e-6

X_OUT, X_T2, X_Q2, X_S, X_PT, X_PV, X_O2, X_T3 = 0, 2, 4, (6, 14), (10, 20), (18, 24), 26, 28
X_TILES = 30
C_LOADS = 16 * (2 * KT + 7 + 10)
O_WRITES = 16 * 2 * HG
PREP_STEPS = 1 + 2 * B + 2 + 4


def max_slot(t):
    return t + (t >= 4) + (t >= 36)


M_SLOTS = (37, 4)


def is_score(i):
    return any(s <= i < s + BLK for s in X_S)


def frees_before(i):
    return sum(1 for j in range(i % 4, i, 4) if not is_score(j))


X_USES = [frees_before(X_TILES + (r - X_TILES) % 4) for r in range(4)]


def free_count(c, i):
    return c * X_USES[i % 4] + frees_before(i)


def build(nc, x, ctxT, wqkv, bqk, bv, wout, bout, wqT, bq2, wkT, bk2, wvT, bv2, woT, bo2,
          wfcT, lnw, lnb, wpT, ident_in, head_mask_in, half_mask_in, ones_bd_in, out):
    qk_scratch = nc.dram_tensor("qk_scratch", (3, 2 * E, T), BF16, kind="Internal").ap()
    v_scratch = nc.dram_tensor("v_scratch", (B, NG, P, KB, P), F32, kind="Internal").ap()
    m_scratch = nc.dram_tensor("m_scratch", (2 * GROUPS, 3, HG, CH), BF16, kind="Internal").ap()
    o_scratch = nc.dram_tensor("o_scratch", (NCH, 2, E, CH), F32, kind="Internal").ap()

    x_v = x.rearrange("(c b p) e -> c p b e", b=BLK, p=P)
    out_v = out.rearrange("(c b p) e -> c p b e", b=BLK, p=P)

    ctx = ExitStack()
    with ctx:
        def sb(name, shape, dt=F32, where=ctx):
            return where.enter_context(nc.sbuf_tensor(name, shape, dt))

        def sem(name):
            return ctx.enter_context(nc.semaphore(name))

        ps = ctx.enter_context(nc.psum_tensor("ps", [P, 8, 512], F32))

        ident = sb("ident", [P, P])
        ident_b = sb("ident_b", [P, P], BF16)
        head_mask = sb("head_mask", [P, 8])
        half_mask = sb("half_mask", [P, 2])
        ones_bd = sb("ones_bd", [P, 32])
        ones = sb("ones", [P, P])
        mhalf = sb("mhalf", [P, 4])
        b_qk = sb("b_qk", [P, 4])
        b_v = sb("b_v", [P, E])
        b_out = sb("b_out", [P, E])
        b_q2 = sb("b_q2", [P, 2])
        b_k2 = sb("b_k2", [P, 2])
        b_v2 = sb("b_v2", [P, E])
        b_o2 = sb("b_o2", [P, E])
        ln_w = sb("ln_w", [P, HT])
        ln_b = sb("ln_b", [P, HT])
        w_out = sb("w_out", [P, KT, E])
        w_q2 = sb("w_q2", [P, KT, E])
        w_o2 = sb("w_o2", [P, KT, E])
        w_fc = sb("w_fc", [P, KT, F])
        w_p = sb("w_p", [P, HT, E])
        abs_sum = sb("abs_sum", [P, 2])
        thr = sb("thr", [P, 3, 2])
        kbd = sb("kbd", [P, B, KT * 8 * CTX])
        vbd = sb("vbd", [P, B, PAIRS * 2 * D])
        touch = sb("touch", [P, 1])
        eps = sb("eps", [P, 4])
        stats = sb("stats", [P, BLK, 6])
        mv = sb("mv", [P, BLK, 2])
        veps = sb("veps", [P, BLK])
        rstd = sb("rstd", [P, BLK])

        ab = ctx.enter_context(ExitStack())
        w_qkv = sb("w_qkv", [P, KT, 3 * E], F32, ab)
        w_k2 = sb("w_k2", [P, KT, E], F32, ab)
        w_v2 = sb("w_v2", [P, KT, E], F32, ab)
        ctx_dup = sb("ctx_dup", [P, KT, B, 2, CTX], F32, ab)
        v2b = sb("v2b", [P, E], F32, ab)
        xa = sb("xa", [P, BLK, E], F32, ab)
        xn_a = sb("xn_a", [P, BLK, E], F32, ab)
        xnT_a = sb("xnT_a", [P, KT, CH], F32, ab)
        parts = sb("parts", [P, 4, 3, CH], BF16, ab)
        rest = sb("rest", [P, 2, CH], F32, ab)
        vx = sb("vx", [P, BLK, H, 32], F32, ab)
        Qs = [sb(f"Qs{i}", [P, HG, S], BF16, ab) for i in range(NG)]
        Ks = [sb(f"Ks{i}", [P, HG, S], BF16, ab) for i in range(NG)]
        Vs = [sb(f"Vs{i}", [P, KB, P], F32, ab) for i in range(NG)]
        prob = sb("prob", [P, 2, 2, 2, CH], F32, ab)
        ot = sb("ot", [P, CH], F32, ab)
        maxes = sb("maxes", [P, 2, 16, 2], F32, ab)
        mrow = sb("mrow", [P, 16], F32, ab)
        mrest = sb("mrest", [P, 16], F32, ab)
        msp = sb("msp", [P, 6, 16], BF16, ab)
        mt = sb("mt", [48, P], BF16, ab)
        ab.close()

        on_raw = sb("on_raw", [P, KT, CH])
        s_raw = sb("s_raw", [P, KT, CH])
        onT = sb("onT", [P, KT, CH])
        x_in = sb("x_in", [P, BLK, E])
        x_b = sb("x_b", [P, BLK, E])
        x1 = sb("x1", [P, BLK, E])
        x1_b = sb("x1_b", [P, BLK, E])
        x2 = sb("x2", [P, BLK, E])
        x2_f = sb("x2_f", [P, BLK, E])
        xn = sb("xn", [P, BLK, E])
        xn2T = sb("xn2T", [P, KT, CH])
        xn3T = sb("xn3T", [P, KT, CH])
        q2T = sb("q2T", [P, KT, CH])
        kcur = sb("kcur", [P, KT * 8 * CTX])
        vcur = sb("vcur", [P, PAIRS * 2 * D])
        nmx = sb("nmx", [P, 2, 8])
        sc = sb("sc", [P, 2, CH])
        pe_ = sb("pe_", [P, BLK, CH])
        pT = sb("pT", [P, 2, 4, CH])
        rs2 = sb("rs2", [P, CH])
        o2T = sb("o2T", [P, KT, CH])
        gl = sb("gl", [P, 2, F])
        fstats = sb("fstats", [P, 2, 2, 6])
        fmv = sb("fmv", [P, 2, 2])
        fveps = sb("fveps", [P, 2])
        frstd = sb("frstd", [P, 2])
        xhat = sb("xhat", [P, BLK, F])
        fT = sb("fT", [P, 2, CH])
        xo = sb("xo", [P, BLK, E])

        a_weights = sem("a_weights")
        c_weights = sem("c_weights")
        const_set = sem("const_set")
        ident_b_set = sem("ident_b_set")
        ones_set = sem("ones_set")
        abs_summed = sem("abs_summed")
        x_loaded = sem("x_loaded")
        stats_done = sem("stats_done")
        mv_ready = sem("mv_ready")
        veps_done = sem("veps_done")
        rstd_ready = sem("rstd_ready")
        xn_ready = sem("xn_ready")
        tr_done = sem("tr_done")
        xT_copied = sem("xT_copied")
        v_mm_done = sem("v_mm_done")
        v_copied = sem("v_copied")
        v_written = sem("v_written")
        qk_mm_done = sem("qk_mm_done")
        part1_done = sem("part1_done")
        rest_done = sem("rest_done")
        part2_done = sem("part2_done")
        parts_ready = sem("parts_ready")
        parts_written = sem("parts_written")
        prep_mm = sem("prep_mm")
        prep_done = sem("prep_done")
        group_loaded = [sem(f"group_loaded{i}") for i in range(NG)]
        max_mm_done = sem("max_mm_done")
        max_reduced = sem("max_reduced")
        m_step = sem("m_step")
        m_split = sem("m_split")
        m_transposed = sem("m_transposed")
        m_copied = sem("m_copied")
        m_written = sem("m_written")
        m_loaded = sem("m_loaded")
        st_done = sem("st_done")
        exp_done = sem("exp_done")
        pv_done = sem("pv_done")
        o_copied = sem("o_copied")
        o_written = sem("o_written")
        on_loaded = sem("on_loaded")
        xc_loaded = sem("xc_loaded")
        recip_done = sem("recip_done")
        o_normed = sem("o_normed")
        xb_ready = sem("xb_ready")
        x1b_ready = sem("x1b_ready")
        kv_copied = sem("kv_copied")
        x2_kept = sem("x2_kept")
        x_done = sem("x_done")
        x_free = [sem(f"x_free{r}") for r in range(4)]
        nmx_done = sem("nmx_done")
        sc_ready = sem("sc_ready")
        p_ready = sem("p_ready")
        fc_done = sem("fc_done")
        gelu_done = sem("gelu_done")
        fstats_done = sem("fstats_done")
        fmv_ready = sem("fmv_ready")
        fveps_done = sem("fveps_done")
        frstd_ready = sem("frstd_ready")
        xhat_done = sem("xhat_done")
        hT_done = sem("hT_done")
        ft_ready = sem("ft_ready")
        acc_done = sem("acc_done")
        out_added = sem("out_added")
        out_written = sem("out_written")

        block = ctx.enter_context(nc.Block())

        @block.sync
        def _(sp):
            for n, (t, d) in enumerate(((ident, ident_in), (w_qkv, wqkv.rearrange("(k p) n -> p k n", p=P)),
                                        (b_qk, bqk), (b_v, bv.partition_broadcast(P)))):
                sp.dma_start(t[:], d).then_inc(a_weights, 16)

            def phase_a(c, last):
                b, kb = c // 2, (c % 2) * BLK
                sp.wait_ge(v_copied, 2 * c + 2)
                for g in range(NG):
                    sp.dma_start(v_scratch[b, g, :, bass.ds(kb, BLK), :],
                                 vx[:, :, g * HG:(g + 1) * HG, :].rearrange("p b h d -> p b (h d)")
                                 ).then_inc(v_written, 16)
                for m in range(4):
                    sp.wait_ge(parts_ready, 4 * c + m + 1)
                    sp.dma_start(qk_scratch[:, m * P:(m + 1) * P, bass.ts(c, CH)].rearrange("s p t -> p s t"),
                                 parts[:, m]).then_inc(parts_written, 16)

            phase_a(0, False)
            with sp.Fori(1, NCH - 1) as c:
                phase_a(c, False)
            phase_a(NCH - 1, True)

            def load_group(b, g):
                for slots, base, dst in ((SLOTS_Q, 0, Qs[g]), (SLOTS_K, E, Ks[g])):
                    for i, part in enumerate(slots):
                        rows = qk_scratch[part, base + g * HG * D:base + (g + 1) * HG * D, bass.ts(b, S)]
                        sp.dma_start(dst[i * D:(i + 1) * D, :, :],
                                     rows.rearrange("(j d) t -> d j t", d=D)).then_inc(group_loaded[g], 16)
                sp.dma_start(Vs[g][:], v_scratch[b, g]).then_inc(group_loaded[g], 16)

            sp.wait_ge(v_written, 16 * NG * NCH)
            sp.wait_ge(parts_written, 16 * 4 * NCH)
            for g in range(3):
                load_group(0, g)

            def m_rows(f, g, qc):
                sp.wait_ge(m_copied, f + 1)
                sp.dma_start(m_scratch[f].rearrange("s j (k q) -> (s j k) q", q=P), mt[:]).then_inc(m_written, 16)
                sp.wait_ge(m_written, 16 * (f + 1))
                sp.dma_start(Qs[g][STACK:ROWS, :, qc * CH:(qc + 1) * CH], m_scratch[f]).then_inc(m_loaded, 16)

            def o_write(G, b, g, qc):
                sp.wait_ge(o_copied, 2 * G + qc + 1)
                for j in range(HG):
                    rows = slice((g * HG + j) * D, (g * HG + j + 1) * D)
                    for kind in range(2):
                        r0 = 32 * j + D * kind
                        sp.dma_start(o_scratch[b * QC + qc, kind, rows, :], ot[r0:r0 + D, :]).then_inc(o_written, 16)

            m_rows(0, 0, 0)

            def phase_b(b, last):
                for g in range(NG):
                    G = b * NG + g
                    if not last or g == 0:
                        sp.wait_ge(pv_done, UNITS * G)
                        load_group(b + (g + 3) // NG, (g + 3) % NG)
                    m_rows(2 * G + 1, g, 1)
                    o_write(G, b, g, 0)
                    if not (last and g == NG - 1):
                        m_rows(2 * G + 2, (g + 1) % NG, 0)
                    o_write(G, b, g, 1)

            phase_b(0, False)
            with sp.Fori(1, B - 1) as b:
                phase_b(b, False)
            phase_b(B - 1, True)

            def load_o(c):
                for kind, dst in enumerate((on_raw, s_raw)):
                    sp.dma_start(dst[:], o_scratch[c, kind].rearrange("(k p) t -> p k t", p=P)).then_inc(on_loaded, 16)

            def load_xc(c):
                sp.dma_start(x_in[:], x_v[c]).then_inc(xc_loaded, 16)

            sp.wait_ge(o_written, O_WRITES * 2 * GROUPS)
            sp.wait_ge(prep_done, PREP_STEPS)
            load_o(0)
            load_xc(0)

            def write_out(c):
                sp.wait_ge(out_added, 2 * c + 2)
                sp.dma_start(out_v[c], xo[:]).then_inc(out_written, 16)

            def phase_c(c, first, last):
                if not last:
                    sp.wait_ge(o_normed, c + 1)
                    load_o(c + 1)
                    sp.wait_ge(xb_ready, c + 1)
                    load_xc(c + 1)
                if not first:
                    write_out(c - 1)

            phase_c(0, True, False)
            phase_c(1, False, False)
            with sp.Fori(2, NCH - 1) as c:
                phase_c(c, False, False)
            phase_c(NCH - 1, False, True)
            write_out(NCH - 1)
            sp.wait_ge(out_written, 16 * NCH)

        @block.gpsimd
        def _(pool):
            pool.dma_start(xa[:], x_v[0]).then_inc(x_loaded, 16)
            pool.memset(ones[:], 1.0).then_inc(const_set, 1)
            pool.memset(mhalf[:], -0.5).then_inc(const_set, 1)
            pool.memset(eps[:], LN_EPS).then_inc(const_set, 1)
            pool.memset(msp[:], 0.0).then_inc(const_set, 1)
            pool.wait_ge(const_set, 4)
            def make_rstd(n):
                pool.wait_ge(mv_ready, n + 1)
                pool.tensor_tensor(veps[:], mv[:, :, 1], eps[:], ALU.add).then_inc(veps_done, 1)
                pool.wait_ge(veps_done, n + 1)
                pool.tensor_tensor(rstd[:], veps[:], mhalf[:], ALU.pow).then_inc(rstd_ready, 1)

            def phase_a(c):
                make_rstd(c)
                pool.wait_ge(xn_ready, c + 1)
                pool.dma_start(xa[:], x_v[c + 1]).then_inc(x_loaded, 16)

            phase_a(0)
            for g in range(NG):
                pool.wait_ge(const_set, 4 + g)
                pool.memset(Ks[g][STACK:ROWS, :, :], 1.0).then_inc(const_set, 1)
            pool.wait_ge(const_set, 4 + NG)
            with pool.Fori(1, NCH - 1) as c:
                phase_a(c)
            make_rstd(NCH - 1)

            def f_rstd(c, blk):
                n = BLK * c + blk
                s = blk % 2
                pool.wait_ge(fmv_ready, n + 1)
                pool.tensor_tensor(fveps[:, s:s + 1], fmv[:, s, 1:2], eps[:, 0:1], ALU.add).then_inc(fveps_done, 1)
                pool.wait_ge(fveps_done, n + 1)
                pool.tensor_tensor(frstd[:, s:s + 1], fveps[:, s:s + 1], mhalf[:, 0:1], ALU.pow).then_inc(frstd_ready, 1)

            def x_plus_b(c):
                pool.wait_ge(xc_loaded, 16 * (c + 1))
                pool.tensor_tensor(x_b[:], x_in[:], b_out[:, None, :].broadcast_to([P, BLK, E]),
                                   ALU.add).then_inc(xb_ready, 1)

            pool.wait_ge(c_weights, C_LOADS)
            pool.wait_ge(prep_done, PREP_STEPS)
            x_plus_b(0)

            def phase_c(c, first, last):
                if not first:
                    f_rstd(c - 1, 0)
                make_rstd(NCH + 2 * c)
                for i in (X_OUT, X_OUT + 1):
                    pool.wait_ge(x_free[i % 4], free_count(c, i) + 1)
                pool.tensor_tensor(x1_b[:], x1[:], b_o2[:, None, :].broadcast_to([P, BLK, E]),
                                   ALU.add).then_inc(x1b_ready, 1)
                b = c // 2
                pool.tensor_copy(kcur[:], kbd[:, b]).then_inc(kv_copied, 1)
                pool.tensor_copy(vcur[:], vbd[:, b]).then_inc(kv_copied, 1)
                if not first:
                    for blk in range(1, BLK):
                        f_rstd(c - 1, blk)
                if not last:
                    x_plus_b(c + 1)
                make_rstd(NCH + 2 * c + 1)

            phase_c(0, True, False)
            with pool.Fori(1, NCH - 1) as c:
                phase_c(c, False, False)
            phase_c(NCH - 1, False, True)
            for blk in range(BLK):
                f_rstd(NCH - 1, blk)

        @block.scalar
        def _(act):
            for h in range(2):
                for k in range(KT):
                    act.dma_start(ctx_dup[:, k, :, h, :],
                                  ctxT[k * P:(k + 1) * P, :].rearrange("p (b t) -> p b t", b=B)).then_inc(c_weights, 16)
            for t, d in ((w_out, wout), (w_q2, wqT), (w_k2, wkT), (w_v2, wvT), (w_o2, woT), (w_fc, wfcT), (w_p, wpT)):
                act.dma_start(t[:], d.rearrange("(k p) n -> p k n", p=P)).then_inc(c_weights, 16)
            for t, d in ((b_q2, bq2), (b_k2, bk2), (ln_w, lnw), (ln_b, lnb), (head_mask, head_mask_in),
                         (half_mask, half_mask_in), (ones_bd, ones_bd_in), (b_out, bout.partition_broadcast(P)),
                         (b_v2, bv2.partition_broadcast(P)), (b_o2, bo2.partition_broadcast(P))):
                act.dma_start(t[:], d).then_inc(c_weights, 16)
            act.wait_ge(a_weights, 16 * 4)
            act.activation(ident_b[:], ident[:], ACT.Copy).then_inc(ident_b_set, 1)

            def xT_copy(c):
                act.wait_ge(qk_mm_done, 4 * c)
                for k in range(KT):
                    act.wait_ge(tr_done, 2 * c + k + 1)
                    act.activation(xnT_a[:, k, :], ps[:, k, :], ACT.Copy).then_inc(xT_copied, 1)

            def part1(c, m):
                act.wait_ge(qk_mm_done, 4 * c + m + 1)
                if m == 0:
                    act.wait_ge(parts_written, 16 * 4 * c)
                act.activation(parts[:, m, 0, :], ps[:, 4 + m, :], ACT.Identity,
                               bias=b_qk[:, m:m + 1]).then_inc(part1_done, 1)

            def part2(c, m):
                act.wait_ge(rest_done, 4 * c + m + 1)
                act.activation(parts[:, m, 1, :], rest[:, m % 2, :], ACT.Copy).then_inc(part2_done, 1)

            def phase_a(c, last):
                part1(c, 0)
                part1(c, 1)
                part2(c, 0)
                part1(c, 2)
                part2(c, 1)
                part1(c, 3)
                if not last:
                    xT_copy(c + 1)
                part2(c, 2)
                part2(c, 3)

            xT_copy(0)
            phase_a(0, False)
            with act.Fori(1, NCH - 1) as c:
                phase_a(c, False)
            phase_a(NCH - 1, True)

            junk = vx[:].rearrange("p b h d -> p (b h d)")
            act.wait_ge(v_written, 16 * NG * NCH)
            act.wait_ge(c_weights, C_LOADS)
            for i, w in enumerate((w_fc, w_p)):
                act.wait_ge(abs_summed, i)
                act.activation(junk, w[:].rearrange("p k n -> p (k n)"), ACT.Abs,
                               accum_out=abs_sum[:, i:i + 1]).then_inc(abs_summed, 1)

            def m_copy(f, qc):
                act.wait_ge(m_transposed, f + 1)
                act.wait_ge(m_written, 16 * f)
                act.activation(mt[:], ps[:, 5 + M_SLOTS[qc] % 3, :].bitcast(BF16)[0:48, 0:P], ACT.Copy).then_inc(m_copied, 1)

            def exps(U, par):
                for h in range(2):
                    act.wait_ge(st_done, 2 * U + h + 1)
                    act.activation(prob[:, par, h].rearrange("p a q -> p (a q)"),
                                   ps[:, 2 * h:2 * h + 2, :].rearrange("p a q -> p (a q)"),
                                   ACT.Exp).then_inc(exp_done, 1)

            act.wait_ge(abs_summed, 2)
            m_copy(0, 0)
            exps(0, 0)

            def phase_b(b, last):
                for g in range(NG):
                    G = b * NG + g
                    end = last and g == NG - 1
                    for s in range(UNITS):
                        U = G * UNITS + s
                        if s == 2:
                            m_copy(2 * G + 1, 1)
                        if s == 10 and not end:
                            m_copy(2 * G + 2, 0)
                        if not (end and s == UNITS - 1):
                            act.wait_ge(pv_done, U)
                            exps(U + 1, (s + 1) % 2)
                        if s % KB == KB - 1:
                            qc = s // KB
                            act.wait_ge(pv_done, U + 1)
                            act.wait_ge(o_written, O_WRITES * (2 * G + qc))
                            act.activation(ot[:], ps[:, 4, :], ACT.Copy).then_inc(o_copied, 1)

            phase_b(0, False)
            with act.Fori(1, B - 1) as b:
                phase_b(b, False)
            phase_b(B - 1, True)

            def x_ready(c, i):
                act.wait_ge(x_done, X_TILES * c + i + 1)

            def x_copy(c, i, dst):
                x_ready(c, i)
                act.activation(dst, ps[:, i % 4, :], ACT.Copy).then_inc(x_free[i % 4], 1)

            def gelu(c, blk):
                act.wait_ge(fc_done, BLK * c + blk + 1)
                act.wait_ge(xhat_done, BLK * c + max(blk - 1, 0))
                act.activation(gl[:, blk % 2, :], ps[:, 4:6, :].rearrange("p a q -> p (a q)"),
                               ACT.Gelu).then_inc(gelu_done, 1)

            def ft_copy(c, t):
                act.wait_ge(hT_done, HT * c + t + 1)
                act.activation(fT[:, t % 2, :], ps[:, 4 + t % 2, :], ACT.Identity,
                               scale=ln_w[:, t:t + 1], bias=ln_b[:, t:t + 1]).then_inc(ft_ready, 1)

            def c_exp(c, m, blk):
                act.wait_ge(sc_ready, 8 * c + 4 * m + blk + 1)
                act.activation(pe_[:, blk, :], sc[:, blk % 2, :], ACT.Exp, scale=0.25).then_inc(p_ready, 1)

            def phase_c(c, first, last):
                def ffn(f, *a):
                    if not first:
                        f(c - 1, *a)
                ffn(gelu, 0)
                ffn(gelu, 1)
                for k in range(KT):
                    x_copy(c, X_T2 + k, xn2T[:, k, :])
                ffn(gelu, 2)
                for m in range(KT):
                    x_ready(c, X_Q2 + m)
                    act.activation(q2T[:, m, :], ps[:, (X_Q2 + m) % 4, :], ACT.Identity,
                                   bias=b_q2[:, m:m + 1]).then_inc(x_free[(X_Q2 + m) % 4], 1)
                ffn(gelu, 3)
                for m in range(KT):
                    for blk in range(BLK):
                        c_exp(c, m, blk)
                    for t in ((0,), (2, 3))[m]:
                        ffn(ft_copy, t)
                    for blk in range(BLK):
                        i = X_PT[m] + blk
                        x_ready(c, i)
                        act.activation(pT[:, m, :, blk * P:(blk + 1) * P],
                                       ps[:, i % 4, :].rearrange("p (r q) -> p r q", r=4),
                                       ACT.Copy).then_inc(x_free[i % 4], 1)
                    ffn(ft_copy, 1 if m == 0 else 4)
                for t in range(5, HT):
                    ffn(ft_copy, t)
                for k in range(KT):
                    x_copy(c, X_T3 + k, xn3T[:, k, :])
                act.wait_ge(out_added, 2 * c)
                act.activation(x2_f[:], x2[:], ACT.Copy).then_inc(x2_kept, 1)

            phase_c(0, True, False)
            phase_c(1, False, False)
            with act.Fori(2, NCH - 1) as c:
                phase_c(c, False, False)
            phase_c(NCH - 1, False, True)
            for blk in range(BLK):
                gelu(NCH - 1, blk)
            for t in range(HT):
                ft_copy(NCH - 1, t)

        @block.vector
        def _(dve):
            dve.memset(vx[:, :, :, D:32], float(E) ** 0.5).then_inc(ones_set, 1)

            def ln_stats(n, src):
                for blk in range(BLK):
                    i = dve.bn_stats(stats[:, blk, :], src[:, blk, :])
                i.then_inc(stats_done, 1)
                dve.wait_ge(stats_done, n + 1)
                dve.tensor_copy(touch[:], stats[:, 0, 0:1])
                for blk in range(BLK):
                    i = dve.bn_aggr(mv[:, blk, :], stats[:, blk, :])
                i.then_inc(mv_ready, 1)

            def ln_apply(n, src, dst):
                dve.wait_ge(rstd_ready, n + 1)
                for blk in range(BLK):
                    i = dve.tensor_scalar(dst[:, blk, :], src[:, blk, :], mv[:, blk, 0:1], rstd[:, blk:blk + 1],
                                          ALU.subtract, ALU.mult)
                i.then_inc(xn_ready, 1)

            def a_stats(c):
                dve.wait_ge(x_loaded, 16 * (c + 1))
                ln_stats(c, xa)

            def a_apply(c):
                dve.wait_ge(tr_done, 2 * c)
                ln_apply(c, xa, xn_a)

            def v_copy(c):
                dve.wait_ge(v_written, 16 * NG * c)
                for i in range(2):
                    dve.wait_ge(v_mm_done, 2 * c + i + 1)
                    dve.tensor_tensor(vx[:, 2 * i:2 * i + 2, :, 0:D],
                                      ps[:, 2 + i, :].rearrange("p (b h d) -> p b h d", b=2, h=H),
                                      b_v[:].rearrange("p (b h d) -> p b h d", b=1, h=H).broadcast_to([P, 2, H, D]),
                                      ALU.add).then_inc(v_copied, 1)

            def rest1(c, m):
                dve.wait_ge(parts_ready, 4 * c + max(m - 1, 0))
                dve.wait_ge(part1_done, 4 * c + m + 1)
                dve.scalar_tensor_tensor(out=rest[:, m % 2, :], in0=ps[:, 4 + m, :], scalar=b_qk[:, m:m + 1],
                                         in1=parts[:, m, 0, :], op0=ALU.add, op1=ALU.subtract).then_inc(rest_done, 1)

            def part3(c, m):
                dve.wait_ge(part2_done, 4 * c + m + 1)
                dve.tensor_tensor(parts[:, m, 2, :], rest[:, m % 2, :], parts[:, m, 1, :],
                                  ALU.subtract).then_inc(parts_ready, 1)

            def phase_a(c, last):
                if not last:
                    a_stats(c + 1)
                v_copy(c)
                rest1(c, 0)
                if not last:
                    a_apply(c + 1)
                rest1(c, 1)
                part3(c, 0)
                rest1(c, 2)
                part3(c, 1)
                rest1(c, 3)
                part3(c, 2)
                part3(c, 3)

            a_stats(0)
            a_apply(0)
            dve.wait_ge(a_weights, 16 * 4)
            dve.wait_ge(ones_set, 1)
            phase_a(0, False)
            with dve.Fori(1, NCH - 1) as c:
                phase_a(c, False)
            phase_a(NCH - 1, True)

            def reduce_tile(G, t):
                dve.wait_ge(max_mm_done, MAXT * G + t + 1)
                qc, i = divmod(t, MAXT // 2)
                dve.tensor_reduce(maxes[:, qc, i // 2, i % 2:i % 2 + 1], ps[:, 5 + max_slot(t) % 3, :], AX.X,
                                  ALU.max).then_inc(max_reduced, 1)

            def split_max(G, qc):
                f = 2 * G + qc
                dve.wait_ge(max_reduced, MAXT * G + (qc + 1) * (MAXT // 2))
                dve.tensor_tensor(mrow[:], maxes[:, qc, :, 0], maxes[:, qc, :, 1], ALU.max).then_inc(m_step, 1)
                dve.wait_ge(m_step, 3 * f + 1)
                dve.wait_ge(m_transposed, f)
                dve.tensor_scalar(msp[:, 0, :], mrow[:], -1.0, None, ALU.mult).then_inc(m_step, 1)
                dve.wait_ge(m_step, 3 * f + 2)
                dve.scalar_tensor_tensor(out=mrest[:], in0=mrow[:], scalar=-1.0, in1=msp[:, 0, :],
                                         op0=ALU.mult, op1=ALU.subtract).then_inc(m_step, 1)
                dve.wait_ge(m_step, 3 * f + 3)
                dve.tensor_copy(msp[:, 1, :], mrest[:]).then_inc(m_split, 1)
                dve.wait_ge(m_split, 2 * f + 1)
                dve.tensor_tensor(msp[:, 2, :], mrest[:], msp[:, 1, :], ALU.subtract).then_inc(m_split, 1)

            for t in range(MAXT):
                reduce_tile(0, t)
                if t == MAXT // 2 - 1:
                    split_max(0, 0)
            split_max(0, 1)

            def phase_b(b, last):
                for g in range(NG - 1 if last else NG):
                    G = b * NG + g + 1
                    for t in range(MAXT):
                        reduce_tile(G, t)
                        if t == MAXT // 2 - 1:
                            split_max(G, 0)
                    split_max(G, 1)

            phase_b(0, False)
            with dve.Fori(1, B - 1) as b:
                phase_b(b, False)
            phase_b(B - 1, True)

            dve.wait_ge(c_weights, C_LOADS)
            n = 0
            dve.wait_ge(prep_mm, 1)
            for m in range(KT):
                src = ps[:, 5, m * B * CTX:(m + 1) * B * CTX].rearrange("p (b t) -> p b t", b=B)
                for h in range(8):
                    i = dve.tensor_scalar(kbd[:, :, (m * 8 + h) * CTX:(m * 8 + h + 1) * CTX], src, b_k2[:, m:m + 1], head_mask[:, h:h + 1],
                                          ALU.add, ALU.mult)
            i.then_inc(prep_done, 1)
            n += 1
            for b in range(B):
                dve.wait_ge(prep_mm, 2 + b // 2)
                dve.tensor_tensor(v2b[:], ps[:, 6 + b // 2, (b % 2) * E:(b % 2 + 1) * E], b_v2[:],
                                  ALU.add).then_inc(prep_done, 1)
                n += 1
                dve.wait_ge(prep_done, n)
                v2v = v2b[:].rearrange("p (r h d) -> p r h d", r=PAIRS, h=2)
                for h in range(2):
                    i = dve.tensor_scalar(vbd[:, b].rearrange("p (r h d) -> p r h d", r=PAIRS, h=2)[:, :, h, :], v2v[:, :, h, :], half_mask[:, h:h + 1], None, ALU.mult)
                i.then_inc(prep_done, 1)
                n += 1
                dve.wait_ge(prep_done, n)
            dve.wait_ge(prep_mm, 4)
            dve.tensor_scalar(thr[:, 0, :], ps[:, 5, 0:2], 1.0 / (E * F), ABS_EPS, ALU.mult, ALU.add).then_inc(prep_done, 1)
            n += 1
            dve.wait_ge(prep_done, n)
            dve.tensor_scalar(thr[:, 1, :], thr[:, 0, :], 0.5, None, ALU.mult)
            dve.tensor_scalar(thr[:, 2, :], thr[:, 0, :], -0.5, None, ALU.mult).then_inc(prep_done, 1)
            n += 1
            dve.wait_ge(prep_done, n)
            neg = vx[:].rearrange("p b h d -> p (b h d)")
            for i, w in enumerate((w_fc, w_p)):
                wf = w[:].rearrange("p k n -> p (k n)")
                dve.tensor_scalar(neg, wf, thr[:, 2, i:i + 1], None, ALU.is_lt).then_inc(prep_done, 1)
                n += 1
                dve.wait_ge(prep_done, n)
                dve.scalar_tensor_tensor(out=wf, in0=wf, scalar=thr[:, 1, i:i + 1], in1=neg,
                                         op0=ALU.is_gt, op1=ALU.subtract).then_inc(prep_done, 1)
                n += 1
                dve.wait_ge(prep_done, n)
            assert n == PREP_STEPS

            def x_ready(c, i):
                dve.wait_ge(x_done, X_TILES * c + i + 1)

            def normalise(c):
                dve.wait_ge(on_loaded, 16 * 2 * (c + 1))
                dve.reciprocal(s_raw[:], s_raw[:]).then_inc(recip_done, 1)
                dve.wait_ge(recip_done, c + 1)
                dve.tensor_tensor(onT[:], on_raw[:], s_raw[:], ALU.mult).then_inc(o_normed, 1)

            def add_tile(c, i, dst, src, k):
                x_ready(c, i)
                dve.tensor_tensor(dst[:, 2 * k:2 * k + 2, :], ps[:, i % 4, :].rearrange("p (b e) -> p b e", b=2),
                                  src[:, 2 * k:2 * k + 2, :], ALU.add).then_inc(x_free[i % 4], 1)

            def scores(c, m, blk, first):
                i = X_S[m] + blk
                s = ps[:, i % 4, :].rearrange("p (h t) -> p h t", h=8)
                x_ready(c, i)
                k = blk % 2
                if not first or 4 * m + blk >= 2:
                    dve.wait_ge(p_ready, 8 * c + 4 * m + blk - 1)
                dve.tensor_reduce(nmx[:, k, :], s, AX.X, ALU.max, negate=True).then_inc(nmx_done, 1)
                dve.wait_ge(nmx_done, 8 * c + 4 * m + blk + 1)
                dve.tensor_tensor(sc[:, k, :].rearrange("p (h t) -> p h t", h=8), s,
                                  nmx[:, k, :, None].broadcast_to([P, 8, CTX]), ALU.add).then_inc(sc_ready, 1)

            def x_norm(c, m):
                i = X_PV[m]
                x_ready(c, i + 1)
                if m == 1:
                    dve.wait_ge(x_free[X_PV[0] % 4], free_count(c, X_PV[0]) + 1)
                dve.reciprocal(rs2[:], ps[:, (i + 1) % 4, :]).then_inc(x_free[(i + 1) % 4], 1)
                dve.wait_ge(x_free[(i + 1) % 4], free_count(c, i + 1) + 1)
                dve.tensor_tensor(o2T[:, m, :], ps[:, i % 4, :], rs2[:], ALU.mult).then_inc(x_free[i % 4], 1)

            def f_stats(c, blk):
                n = BLK * c + blk
                k = blk % 2
                dve.wait_ge(gelu_done, n + 1)
                for h in range(2):
                    i = dve.bn_stats(fstats[:, k, h, :], gl[:, k, h * 512:(h + 1) * 512])
                i.then_inc(fstats_done, 1)
                dve.wait_ge(fstats_done, n + 1)
                dve.tensor_copy(touch[:], fstats[:, k, 0, 0:1])
                dve.bn_aggr(fmv[:, k, :], fstats[:, k, :, :]).then_inc(fmv_ready, 1)

            def f_apply(c, blk):
                k = blk % 2
                dve.wait_ge(frstd_ready, BLK * c + blk + 1)
                dve.tensor_scalar(xhat[:, blk, :], gl[:, k, :], fmv[:, k, 0:1], frstd[:, k:k + 1],
                                  ALU.subtract, ALU.mult).then_inc(xhat_done, 1)

            def f_out(c):
                dve.wait_ge(acc_done, c + 1)
                dve.wait_ge(x2_kept, c + 1)
                dve.wait_ge(out_written, 16 * c)
                for i in range(2):
                    dve.tensor_tensor(xo[:, 2 * i:2 * i + 2, :], ps[:, 6 + i, :].rearrange("p (b e) -> p b e", b=2),
                                      x2_f[:, 2 * i:2 * i + 2, :], ALU.add).then_inc(out_added, 1)

            normalise(0)

            def phase_c(c, first, last):
                def ffn(f, *a):
                    if not first:
                        f(c - 1, *a)
                dve.wait_ge(xb_ready, c + 1)
                add_tile(c, X_OUT, x1, x_b, 0)
                ffn(f_stats, 0)
                add_tile(c, X_OUT + 1, x1, x_b, 1)
                for i in (X_OUT, X_OUT + 1):
                    dve.wait_ge(x_free[i % 4], free_count(c, i) + 1)
                ln_stats(NCH + 2 * c, x1)
                ffn(f_apply, 0)
                ln_apply(NCH + 2 * c, x1, xn)
                ffn(f_stats, 1)
                ffn(f_apply, 1)
                ffn(f_stats, 2)
                ffn(f_apply, 2)
                ffn(f_stats, 3)
                scores(c, 0, 0, first)
                ffn(f_apply, 3)
                for blk in range(1, BLK):
                    scores(c, 0, blk, first)
                for blk in range(BLK):
                    scores(c, 1, blk, first)
                x_norm(c, 0)
                x_norm(c, 1)
                if not last:
                    normalise(c + 1)
                dve.wait_ge(x1b_ready, c + 1)
                if not first:
                    dve.wait_ge(x2_kept, c)
                for k in range(2):
                    add_tile(c, X_O2 + k, x2, x1_b, k)
                for i in (X_O2, X_O2 + 1):
                    dve.wait_ge(x_free[i % 4], free_count(c, i) + 1)
                ln_stats(NCH + 2 * c + 1, x2)
                ln_apply(NCH + 2 * c + 1, x2, xn)
                ffn(f_out)

            phase_c(0, True, False)
            phase_c(1, False, False)
            with dve.Fori(2, NCH - 1) as c:
                phase_c(c, False, False)
            phase_c(NCH - 1, False, True)
            for blk in range(BLK):
                f_stats(NCH - 1, blk)
                f_apply(NCH - 1, blk)
            f_out(NCH - 1)

        @block.tensor
        def _(pe):
            def mm(o, lhsT, rhs, k, n, **kw):
                return pe.matmul(o, lhsT, rhs, start=(k == 0), stop=(k == n - 1), **kw)

            def a_transpose(c):
                pe.wait_ge(xn_ready, c + 1)
                pe.wait_ge(xT_copied, 2 * c)
                for k in range(KT):
                    for blk in range(BLK):
                        i = pe.transpose(ps[:, k, blk * P:(blk + 1) * P], xn_a[:, blk, k * P:(k + 1) * P], ident[:])
                    i.then_inc(tr_done, 1)

            def a_v(c):
                pe.wait_ge(xT_copied, 2 * c + 2)
                pe.wait_ge(v_copied, 2 * c)
                for blk in range(BLK):
                    for k in range(KT):
                        i = mm(ps[:, 2 + blk // 2, (blk % 2) * E:(blk % 2 + 1) * E],
                               xnT_a[:, k, blk * P:(blk + 1) * P], w_qkv[:, k, 2 * E:3 * E], k, KT)
                    if blk % 2:
                        i.then_inc(v_mm_done, 1)

            def a_qk(c, m):
                if m == 0:
                    pe.wait_ge(rest_done, 4 * c)
                for k in range(KT):
                    i = mm(ps[:, 4 + m, :], w_qkv[:, k, m * P:(m + 1) * P], xnT_a[:, k, :], k, KT)
                i.then_inc(qk_mm_done, 1)

            def phase_a(c, last):
                a_v(c)
                for m in range(3):
                    a_qk(c, m)
                if not last:
                    a_transpose(c + 1)
                a_qk(c, 3)

            pe.wait_ge(a_weights, 16 * 4)
            pe.wait_ge(const_set, 4)
            pe.wait_ge(ident_b_set, 1)
            a_transpose(0)
            phase_a(0, False)
            with pe.Fori(1, NCH - 1) as c:
                phase_a(c, False)
            phase_a(NCH - 1, True)

            def prepare(n):
                if n == 0:
                    pe.wait_ge(c_weights, C_LOADS)
                    pe.wait_ge(max_reduced, MAXT * GROUPS)
                    pe.wait_ge(m_copied, 2 * GROUPS)
                    for m in range(KT):
                        for k in range(KT):
                            i = mm(ps[:, 5, m * B * CTX:(m + 1) * B * CTX].rearrange("p (b t) -> p b t", b=B),
                                   w_k2[:, k, m * P:(m + 1) * P], ctx_dup[:, k, :, 0, :], k, KT)
                elif n <= 2:
                    for b in (2 * n - 2, 2 * n - 1):
                        for k in range(KT):
                            i = mm(ps[:, 5 + n, (b % 2) * E:(b % 2 + 1) * E],
                                   ctx_dup[:, k, b, :, :].rearrange("p c t -> p (c t)"), w_v2[:, k, :], k, KT)
                else:
                    pe.wait_ge(abs_summed, 2)
                    pe.wait_ge(prep_done, 1)
                    i = pe.matmul(ps[:, 5, 0:2], ones[:], abs_sum[:], start=True, stop=True)
                i.then_inc(prep_mm, 1)

            pe.wait_ge(rest_done, 4 * NCH)

            def slot_free(G, k, first):
                k -= 3
                if k in M_SLOTS:
                    f = 2 * G + (0 if k == M_SLOTS[0] else -1)
                    if not (first and k == M_SLOTS[1]):
                        pe.wait_ge(m_copied, f + 1)
                elif k >= 0:
                    t = [max_slot(t) for t in range(MAXT)].index(k)
                    pe.wait_ge(max_reduced, MAXT * G + t + 1)
                elif not first:
                    pe.wait_ge(max_reduced, MAXT * G + k + 1)

            def max_tile(G, g, t, first=False):
                qc, i = divmod(t, MAXT // 2)
                j, blk, half = i // 8, (i % 8) // 2, i % 2
                q0 = qc * CH + blk * P
                slot_free(G, max_slot(t), first)
                pe.matmul(ps[:, 5 + max_slot(t) % 3, :], Qs[g][0:STACK, j, q0:q0 + P],
                          Ks[g][0:STACK, j, half * 512:(half + 1) * 512], start=True, stop=True).then_inc(max_mm_done, 1)

            def max_transpose(G, f, qc, last=False):
                k = M_SLOTS[qc]
                if last:
                    pe.wait_ge(max_reduced, MAXT * GROUPS)
                else:
                    slot_free(G, k, False)
                pe.wait_ge(m_split, 2 * f + 2)
                pe.transpose(ps[:, 5 + k % 3, :].bitcast(BF16)[0:96, 0:P], msp[:].rearrange("p s i -> p (s i)"),
                             ident_b[:]).then_inc(m_transposed, 1)

            def scores(U, g, s, h, free=True):
                qc, kb = divmod(s, KB)
                if free:
                    pe.wait_ge(exp_done, 2 * U + h - 1)
                for j in (2 * h, 2 * h + 1):
                    i = pe.matmul(ps[:, j, :], Ks[g][0:ROWS, j, kb * P:(kb + 1) * P],
                                  Qs[g][0:ROWS, j, qc * CH:(qc + 1) * CH], start=True, stop=True)
                i.then_inc(st_done, 1)

            def values(G, g, U, s):
                qc, kb = divmod(s, KB)
                pe.wait_ge(exp_done, 2 * U + 2)
                if kb == 0:
                    pe.wait_ge(o_copied, 2 * G + qc)
                for j in range(HG):
                    i = pe.matmul(ps[32 * j:32 * j + 32, 4, :], Vs[g][:, kb, 32 * j:32 * j + 32],
                                  prob[:, s % 2, j // 2, j % 2, :], start=(kb == 0), stop=(kb == KB - 1))
                i.then_inc(pv_done, 1)

            pe.wait_ge(group_loaded[0], GROUP_LOADS)
            pe.wait_ge(const_set, 4 + NG)
            for t in range(MAXT):
                if t == 36:
                    max_transpose(0, 0, 0)
                max_tile(0, 0, t, True)
            pe.wait_ge(m_loaded, 16)
            scores(0, 0, 0, 0, False)
            scores(0, 0, 0, 1, False)

            def phase_b(b, last):
                for g in range(NG):
                    G = b * NG + g
                    end = last and g == NG - 1
                    g1 = (g + 1) % NG
                    for s in range(UNITS):
                        U = G * UNITS + s
                        if s == 0 and not end:
                            pe.wait_ge(group_loaded[g1], GROUP_LOADS * (b + (g + 1) // NG + 1))
                        if s == 1:
                            max_transpose(G + 1, 2 * G + 1, 1, end)
                        if s == 9 and not end:
                            max_transpose(G + 1, 2 * G + 2, 0)
                        if s == KB - 1:
                            pe.wait_ge(m_loaded, 16 * (2 * G + 2))
                        if s == UNITS - 1 and not end:
                            pe.wait_ge(m_loaded, 16 * (2 * G + 3))
                        for h in range(2):
                            if not end:
                                max_tile(G + 1, g1, 4 * s + h)
                            if not (end and s == UNITS - 1):
                                nxt = (g1, 0) if s == UNITS - 1 else (g, s + 1)
                                scores(U + 1, nxt[0], nxt[1], h)
                        if not end:
                            max_tile(G + 1, g1, 4 * s + 2)
                        values(G, g, U, s)
                        if end and s % 2 == 0 and 4 <= s < 12:
                            prepare(s // 2 - 2)
                        if not end:
                            max_tile(G + 1, g1, 4 * s + 3)

            phase_b(0, False)
            with pe.Fori(1, B - 1) as b:
                phase_b(b, False)
            phase_b(B - 1, True)

            pe.wait_ge(o_copied, 2 * GROUPS)
            pe.wait_ge(max_reduced, MAXT * GROUPS)
            pe.wait_ge(m_copied, 2 * GROUPS)

            def x_bank(c, i):
                before = i - 4
                if is_score(before):
                    m = 0 if before < X_S[1] else 1
                    pe.wait_ge(sc_ready, 8 * c + 4 * m + before - X_S[m] + 1)
                else:
                    pe.wait_ge(x_free[i % 4], free_count(c, i))
                return i % 4

            def pair_of_blocks(c, i, lhs, w):
                for t in range(2):
                    r = x_bank(c, i + t)
                    for h in range(2):
                        blk = 2 * t + h
                        for k in range(KT):
                            n = mm(ps[:, r, h * E:(h + 1) * E], lhs[:, k, blk * P:(blk + 1) * P], w[:, k, :], k, KT)
                    n.then_inc(x_done, 1)
                    yield

            def transposes(c, i):
                for k in range(KT):
                    r = x_bank(c, i + k)
                    for blk in range(BLK):
                        n = pe.transpose(ps[:, r, blk * P:(blk + 1) * P], xn[:, blk, k * P:(k + 1) * P], ident[:])
                    n.then_inc(x_done, 1)

            def ready(c, i):
                pe.wait_ge(x_free[i % 4], free_count(c, i) + 1)

            def q2(c):
                for k in range(KT):
                    ready(c, X_T2 + k)
                for m in range(KT):
                    r = x_bank(c, X_Q2 + m)
                    for k in range(KT):
                        n = mm(ps[:, r, :], w_q2[:, k, m * P:(m + 1) * P], xn2T[:, k, :], k, KT)
                    n.then_inc(x_done, 1)

            def x_scores(c, m):
                if m == 0:
                    pe.wait_ge(kv_copied, 2 * c + 2)
                    ready(c, X_Q2)
                else:
                    ready(c, X_Q2 + 1)
                for blk in range(BLK):
                    r = x_bank(c, X_S[m] + blk)
                    pe.matmul(ps[:, r, :], q2T[:, m, blk * P:(blk + 1) * P], kcur[:, m * 8 * CTX:(m + 1) * 8 * CTX],
                              start=True, stop=True).then_inc(x_done, 1)

            def x_pT(c, m):
                for blk in range(BLK):
                    r = x_bank(c, X_PT[m] + blk)
                    pe.wait_ge(p_ready, 8 * c + 4 * m + blk + 1)
                    for pr in range(4):
                        n = pe.transpose(ps[:, r, pr * P:(pr + 1) * P], pe_[:, blk, pr * P:(pr + 1) * P], ident[:])
                    n.then_inc(x_done, 1)

            def x_values(c, m):
                for blk in range(BLK):
                    ready(c, X_PT[m] + blk)
                for t in range(2):
                    r = x_bank(c, X_PV[m] + t)
                    for pr in range(4):
                        n = pe.matmul(ps[32 * pr:32 * pr + 32, r, :], vcur[:, (4 * m + pr) * 32:(4 * m + pr + 1) * 32] if t == 0 else ones_bd[:],
                                      pT[:, m, pr, :], start=True, stop=True)
                    n.then_inc(x_done, 1)

            def fc(c, blk):
                if blk == 0:
                    pe.wait_ge(x_free[X_T3 % 4], X_USES[X_T3 % 4] * (c + 1))
                    pe.wait_ge(x_free[(X_T3 + 1) % 4], X_USES[(X_T3 + 1) % 4] * (c + 1))
                    pe.wait_ge(ft_ready, HT * c)
                else:
                    pe.wait_ge(gelu_done, BLK * c + blk)
                for h in range(2):
                    for k in range(KT):
                        i = mm(ps[:, 4 + h, :], xn3T[:, k, blk * P:(blk + 1) * P], w_fc[:, k, h * 512:(h + 1) * 512], k, KT)
                i.then_inc(fc_done, 1)

            def f_tile(c, t):
                if t < HT:
                    if t == 0:
                        pe.wait_ge(xhat_done, BLK * (c + 1))
                    elif t >= 2:
                        pe.wait_ge(ft_ready, HT * c + t - 1)
                    for blk in range(BLK):
                        i = pe.transpose(ps[:, 4 + t % 2, blk * P:(blk + 1) * P], xhat[:, blk, t * P:(t + 1) * P], ident[:])
                    i.then_inc(hT_done, 1)
                if t >= 1:
                    pe.wait_ge(ft_ready, HT * c + t)
                    if t == 1:
                        pe.wait_ge(out_added, 2 * c)
                    for blk in range(BLK):
                        i = pe.matmul(ps[:, 6 + blk // 2, (blk % 2) * E:(blk % 2 + 1) * E],
                                      fT[:, (t - 1) % 2, blk * P:(blk + 1) * P], w_p[:, t - 1, :],
                                      start=(t == 1 and blk % 2 == 0), stop=(t == HT), skip_group_check=True)
                    if t == HT:
                        i.then_inc(acc_done, 1)

            def phase_c(c, first, last):
                def ffn(f, *a):
                    if not first:
                        f(c - 1, *a)
                pe.wait_ge(o_normed, c + 1)
                tiles = pair_of_blocks(c, X_OUT, onT, w_out)
                next(tiles)
                ffn(fc, 0)
                next(tiles)
                ffn(fc, 1)
                pe.wait_ge(xn_ready, NCH + 2 * c + 1)
                transposes(c, X_T2)
                ffn(fc, 2)
                q2(c)
                ffn(fc, 3)
                x_scores(c, 0)
                ffn(f_tile, 0)
                x_pT(c, 0)
                ffn(f_tile, 1)
                x_scores(c, 1)
                ffn(f_tile, 2)
                x_values(c, 0)
                ffn(f_tile, 3)
                x_pT(c, 1)
                ffn(f_tile, 4)
                x_values(c, 1)
                ffn(f_tile, 5)
                ffn(f_tile, 6)
                for m in range(KT):
                    ready(c, X_PV[m])
                for _ in pair_of_blocks(c, X_O2, o2T, w_o2):
                    pass
                ffn(f_tile, 7)
                ffn(f_tile, 8)
                pe.wait_ge(xn_ready, NCH + 2 * c + 2)
                transposes(c, X_T3)

            phase_c(0, True, False)
            phase_c(1, False, False)
            with pe.Fori(2, NCH - 1) as c:
                phase_c(c, False, False)
            phase_c(NCH - 1, False, True)
            for blk in range(BLK):
                fc(NCH - 1, blk)
            for t in range(HT + 1):
                f_tile(NCH - 1, t)


def kernel(x, ctx_1024, L0_attn_W_qkv, L0_attn_b_qkv, L0_attn_W_out, L0_attn_b_out,
           L0_xattn_Wq, L0_xattn_bq, L0_xattn_Wk, L0_xattn_bk, L0_xattn_Wv, L0_xattn_bv, L0_xattn_Wo, L0_xattn_bo,
           L0_ffn_W_fc, L0_ffn_ln_w, L0_ffn_ln_b, L0_ffn_W_proj):
    import numpy as np
    import concourse.bacc as bacc
    from concourse.bass_utils import run_bass_kernel_spmd

    def columns(v):
        return np.asarray(v).reshape(-1, P).T

    rows = np.arange(P)[:, None]
    arrays = {
        "x": np.asarray(x).reshape(T, E),
        "ctxT": np.asarray(ctx_1024).reshape(B * CTX, E).T,
        "wqkv": L0_attn_W_qkv, "bqk": columns(np.asarray(L0_attn_b_qkv)[:2 * E]), "bv": np.asarray(L0_attn_b_qkv)[2 * E:],
        "wout": L0_attn_W_out, "bout": L0_attn_b_out,
        "wqT": np.asarray(L0_xattn_Wq).T, "bq2": columns(L0_xattn_bq),
        "wkT": np.asarray(L0_xattn_Wk).T, "bk2": columns(L0_xattn_bk),
        "wvT": np.asarray(L0_xattn_Wv).T, "bv2": L0_xattn_bv,
        "woT": np.asarray(L0_xattn_Wo).T, "bo2": L0_xattn_bo,
        "wfcT": np.asarray(L0_ffn_W_fc).T, "lnw": columns(L0_ffn_ln_w), "lnb": columns(L0_ffn_ln_b),
        "wpT": np.asarray(L0_ffn_W_proj).T,
        "ident": np.eye(P, dtype=np.float32),
        "head_mask": (rows // D == np.arange(8)[None]).astype(np.float32),
        "half_mask": (rows // CTX == np.arange(2)[None]).astype(np.float32),
        "ones_bd": (rows // CTX == (np.arange(32) // D)[None]).astype(np.float32),
    }
    arrays = {f"in_{n}": np.ascontiguousarray(a) for n, a in arrays.items()}
    nc = bacc.Bacc("TRN2", target_bir_lowering=False, num_devices=1)
    args = [nc.dram_tensor(n, a.shape, mybir.dt.from_np(a.dtype), kind="ExternalInput").ap() for n, a in arrays.items()]
    out = nc.dram_tensor("out", (T, E), F32, kind="ExternalOutput").ap()
    build(nc, *args, out)
    r = run_bass_kernel_spmd(nc, [arrays], core_ids=[0])
    return r.results[0]["out"].reshape(B, S, E)
```

```python
from contextlib import ExitStack

import concourse.bass as bass
from concourse import mybir

F32 = mybir.dt.float32
BF16 = mybir.dt.bfloat16
F32R = mybir.dt.float32r
ALU = mybir.AluOpType
ACT = mybir.ActivationFunctionType
AX = mybir.AxisListType

P = 128
B, S, E = 4, 1024, 256
H, D = 16, 16
CTX = 64
F = 1024
T = B * S
CH = 512
NCH = T // CH
BLK = CH // P
KT = E // P
HG = 4
NG = H // HG
GROUPS = B * NG
KB = S // P
QC = S // CH
MSLOTS = 66
UNITS = QC * KB
MAXT = UNITS * 4
SLOTS_Q = (0, 0, 1, 1, 0, 2)
SLOTS_K = (0, 1, 0, 1, 2, 0)
STACK = len(SLOTS_Q) * D
ROWS = STACK + 3
GROUP_LOADS = 16 * (2 * len(SLOTS_Q) + 1)
HT = F // P
PAIRS = H // 2
LN_EPS = 1e-5
ABS_EPS = 1e-6

X_T2, X_Q2, X_S, X_PT, X_PV, X_O2, X_OUT, X_T3 = 0, 2, (4, 12), (8, 18), (16, 22), 24, (26, 29), 27
X_TILES = 30
X_BEFORE = [sum(i % 4 == r for i in X_OUT) for r in range(4)]
C_LOADS = 16 * (2 * KT + 7 + 10)
O_WRITES = 16 * (HG + 1)
PREP_STEPS = 1 + 2 * B + 2 + 4 + 2
SQ = QC * CH * H // P


def max_slot(t):
    return t + (t >= 8) + (t >= 40)


M_SLOTS = (41, 8)


def is_score(i):
    return any(s <= i < s + BLK for s in X_S)


def frees_before(i):
    return sum(1 for j in range(i % 4, i, 4) if not is_score(j))


X_USES = [frees_before(X_TILES + (r - X_TILES) % 4) for r in range(4)]


def free_count(c, i):
    return c * X_USES[i % 4] + frees_before(i) + X_BEFORE[i % 4]


def done_count(c, i):
    missing = sum(j <= i for j in X_OUT) if isinstance(c, int) and c == NCH - 1 else 0
    return X_TILES * c + i + 1 + len(X_OUT) - missing


def x1_count(c, k):
    r = X_OUT[k] % 4
    return c * X_USES[r] + X_BEFORE[r]


def build(nc, x, ctxT, wqkv, bqk, bv, wout, bout, wqT, bq2, wkT, bk2, wvT, bv2, woT, bo2,
          wfcT, lnw, lnb, wpT, ident_in, head_mask_in, half_mask_in, ones_bd_in, out):
    qk_scratch = nc.dram_tensor("qk_scratch", (3, 2 * E, T), BF16, kind="Internal").ap()
    v_scratch = nc.dram_tensor("v_scratch", (B, NG, P, KB, P), F32, kind="Internal").ap()
    m_scratch = nc.dram_tensor("m_scratch", (2 * GROUPS, 3, HG, CH), BF16, kind="Internal").ap()
    o_scratch = nc.dram_tensor("o_scratch", (NCH, E, CH), F32, kind="Internal").ap()
    s_scratch = nc.dram_tensor("s_scratch", (B, H, QC, CH), F32, kind="Internal").ap()
    r_scratch = nc.dram_tensor("r_scratch", (B, H, QC, CH), F32, kind="Internal").ap()

    x_v = x.rearrange("(c b p) e -> c p b e", b=BLK, p=P)
    out_v = out.rearrange("(c b p) e -> c p b e", b=BLK, p=P)

    ctx = ExitStack()
    with ctx:
        def sb(name, shape, dt=F32, where=ctx):
            return where.enter_context(nc.sbuf_tensor(name, shape, dt))

        def sem(name):
            return ctx.enter_context(nc.semaphore(name))

        ps = ctx.enter_context(nc.psum_tensor("ps", [P, 8, 512], F32))

        ident = sb("ident", [P, P])
        ident_b = sb("ident_b", [P, P], BF16)
        head_mask = sb("head_mask", [P, 8])
        half_mask = sb("half_mask", [P, 2])
        ones_bd = sb("ones_bd", [P, 32])
        ones = sb("ones", [P, P])
        mhalf = sb("mhalf", [P, 4])
        b_qk = sb("b_qk", [P, 4])
        b_v = sb("b_v", [P, E])
        b_out = sb("b_out", [P, E])
        b_q2 = sb("b_q2", [P, 2])
        b_k2 = sb("b_k2", [P, 2])
        b_v2 = sb("b_v2", [P, E])
        b_o2 = sb("b_o2", [P, E])
        ln_w = sb("ln_w", [P, HT])
        ln_b = sb("ln_b", [P, HT])
        w_out = sb("w_out", [P, KT, E])
        w_q2 = sb("w_q2", [P, KT, E])
        w_o2 = sb("w_o2", [P, KT, E])
        t_fc = sb("t_fc", [P, KT, F])
        t_p = sb("t_p", [P, HT, E])
        b_f = sb("b_f", [P, E])
        s_c = sb("s_c", [P, B, SQ])
        abs_sum = sb("abs_sum", [P, 2])
        thr = sb("thr", [P, 3, 2])
        kbd = sb("kbd", [P, B, KT * 8 * CTX])
        vbd = sb("vbd", [P, B, PAIRS * 2 * D])
        touch = sb("touch", [P, 1])
        eps = sb("eps", [P, 4])
        stats = sb("stats", [P, 2, BLK, 6])
        mv = sb("mv", [P, 2, BLK, 2])
        veps = sb("veps", [P, 2, BLK])
        rstd = sb("rstd", [P, 2, BLK])

        ab = ctx.enter_context(ExitStack())
        w_fc = sb("w_fc", [P, KT, F], F32, ab)
        w_p = sb("w_p", [P, HT, E], F32, ab)
        w_qkv = sb("w_qkv", [P, KT, 3 * E], F32, ab)
        w_k2 = sb("w_k2", [P, KT, E], F32, ab)
        w_v2 = sb("w_v2", [P, KT, E], F32, ab)
        ctx_dup = sb("ctx_dup", [P, KT, B, 2, CTX], F32, ab)
        v2b = sb("v2b", [P, E], F32, ab)
        xa = sb("xa", [P, BLK, E], F32, ab)
        xn_a = sb("xn_a", [P, BLK, E], F32, ab)
        xnT_a = sb("xnT_a", [P, 2, KT, CH], F32, ab)
        vx = sb("vx", [P, BLK, H, 32], F32, ab)
        Qs = [sb(f"Qs{i}", [P, HG, S], BF16, ab) for i in range(NG)]
        Ks = [sb(f"Ks{i}", [P, HG, S], BF16, ab) for i in range(NG)]
        Vs = [sb(f"Vs{i}", [P, KB, P], F32, ab) for i in range(NG)]
        a_only = ab.enter_context(ExitStack())
        parts = sb("parts", [P, 4, 3, CH], BF16, a_only)
        rest = sb("rest", [P, 2, CH], F32, a_only)
        a_only.close()
        prob = sb("prob", [P, 2, 2, 2, CH], F32, ab)
        ot = sb("ot", [P, CH], F32, ab)
        maxes = sb("maxes", [P, 2, 16, 2], F32, ab)
        mrow = sb("mrow", [P, 16], F32, ab)
        mrest = sb("mrest", [P, 16], F32, ab)
        msp = sb("msp", [P, 6, 16], BF16, ab)
        mt = sb("mt", [48, P], BF16, ab)
        ab.close()

        on_raw = sb("on_raw", [P, KT, CH])
        r_raw = sb("r_raw", [P, KT, CH])
        onT = sb("onT", [P, KT, CH])
        x_in = sb("x_in", [P, BLK, E])
        x_b = sb("x_b", [P, BLK, E])
        x1 = sb("x1", [P, BLK, E])
        x1_b = sb("x1_b", [P, BLK, E])
        x2 = sb("x2", [P, BLK, E])
        x2_f = sb("x2_f", [P, BLK, E])
        xn_1 = sb("xn_1", [P, BLK, E])
        xn_2 = sb("xn_2", [P, BLK, E])
        xn2T = sb("xn2T", [P, KT, CH])
        xn3T = sb("xn3T", [P, 2, KT, CH])
        q2T = sb("q2T", [P, KT, CH])
        kcur = sb("kcur", [P, KT * 8 * CTX])
        vcur = sb("vcur", [P, PAIRS * 2 * D])
        nmx = sb("nmx", [P, 2, 8])
        sc = sb("sc", [P, 2, CH])
        pe_ = sb("pe_", [P, BLK, CH])
        pT = sb("pT", [P, 2, 4, CH])
        rs2 = sb("rs2", [P, CH])
        o2T = sb("o2T", [P, KT, CH])
        gl = sb("gl", [P, 2, F])
        fstats = sb("fstats", [P, 2, 2, 6])
        fmv = sb("fmv", [P, 2, 2])
        fveps = sb("fveps", [P, 2])
        frstd = sb("frstd", [P, 2])
        xhat = sb("xhat", [P, BLK, F])
        fT = sb("fT", [P, 2, 2, CH])
        xo = sb("xo", [P, BLK, E])

        a_weights = sem("a_weights")
        c_weights = sem("c_weights")
        const_set = sem("const_set")
        ident_b_set = sem("ident_b_set")
        ones_set = sem("ones_set")
        abs_summed = sem("abs_summed")
        x_loaded = sem("x_loaded")
        stats_done = sem("stats_done")
        mv_ready = sem("mv_ready")
        veps_done = sem("veps_done")
        rstd_ready = sem("rstd_ready")
        xn_ready = sem("xn_ready")
        tr_done = sem("tr_done")
        xT_copied = sem("xT_copied")
        v_mm_done = sem("v_mm_done")
        v_copied = sem("v_copied")
        v_written = sem("v_written")
        qk_mm_done = sem("qk_mm_done")
        part1_done = sem("part1_done")
        rest_done = sem("rest_done")
        part2_done = sem("part2_done")
        parts_ready = sem("parts_ready")
        parts_written = sem("parts_written")
        prep_mm = sem("prep_mm")
        prep_done = sem("prep_done")
        group_loaded = [sem(f"group_loaded{i}") for i in range(NG)]
        max_mm_done = sem("max_mm_done")
        max_reduced = sem("max_reduced")
        m_step = sem("m_step")
        m_split = sem("m_split")
        m_transposed = sem("m_transposed")
        m_copied = sem("m_copied")
        m_written = sem("m_written")
        m_loaded = sem("m_loaded")
        st_done = sem("st_done")
        exp_done = sem("exp_done")
        pv_done = sem("pv_done")
        o_copied = sem("o_copied")
        o_written = sem("o_written")
        on_loaded = sem("on_loaded")
        xc_loaded = sem("xc_loaded")
        s_loaded = sem("s_loaded")
        recip_done = sem("recip_done")
        r_written = sem("r_written")
        o_normed = sem("o_normed")
        xb_ready = sem("xb_ready")
        x1b_ready = sem("x1b_ready")
        kv_copied = sem("kv_copied")
        x2_kept = sem("x2_kept")
        x_done = sem("x_done")
        x_free = [sem(f"x_free{r}") for r in range(4)]
        nmx_done = sem("nmx_done")
        sc_ready = sem("sc_ready")
        p_ready = sem("p_ready")
        fc_done = sem("fc_done")
        gelu_done = sem("gelu_done")
        fstats_done = sem("fstats_done")
        fmv_ready = sem("fmv_ready")
        fveps_done = sem("fveps_done")
        frstd_ready = sem("frstd_ready")
        xhat_done = sem("xhat_done")
        hT_done = sem("hT_done")
        xh_high = sem("xh_high")
        fh_ready = sem("fh_ready")
        ft_ready = sem("ft_ready")
        acc_done = sem("acc_done")
        out_added = sem("out_added")
        out_written = sem("out_written")

        block = ctx.enter_context(nc.Block())

        @block.sync
        def _(sp):
            for n, (t, d) in enumerate(((ident, ident_in), (w_qkv, wqkv.rearrange("(k p) n -> p k n", p=P)),
                                        (b_qk, bqk), (b_v, bv.partition_broadcast(P)))):
                sp.dma_start(t[:], d).then_inc(a_weights, 16)

            def phase_a(c, last):
                b, kb = c // 2, (c % 2) * BLK
                sp.wait_ge(v_copied, 2 * c + 2)
                for g in range(NG):
                    sp.dma_start(v_scratch[b, g, :, bass.ds(kb, BLK), :],
                                 vx[:, :, g * HG:(g + 1) * HG, :].rearrange("p b h d -> p b (h d)")
                                 ).then_inc(v_written, 16)
                for m in range(4):
                    sp.wait_ge(parts_ready, 4 * c + m + 1)
                    sp.dma_start(qk_scratch[:, m * P:(m + 1) * P, bass.ts(c, CH)].rearrange("s p t -> p s t"),
                                 parts[:, m]).then_inc(parts_written, 16)

            phase_a(0, False)
            with sp.Fori(1, NCH - 1) as c:
                phase_a(c, False)
            phase_a(NCH - 1, True)

            def load_group(b, g):
                for slots, base, dst in ((SLOTS_Q, 0, Qs[g]), (SLOTS_K, E, Ks[g])):
                    for i, part in enumerate(slots):
                        rows = qk_scratch[part, base + g * HG * D:base + (g + 1) * HG * D, bass.ts(b, S)]
                        sp.dma_start(dst[i * D:(i + 1) * D, :, :],
                                     rows.rearrange("(j d) t -> d j t", d=D)).then_inc(group_loaded[g], 16)
                sp.dma_start(Vs[g][:], v_scratch[b, g]).then_inc(group_loaded[g], 16)

            sp.wait_ge(v_written, 16 * NG * NCH)
            sp.wait_ge(parts_written, 16 * 4 * NCH)
            for g in range(3):
                load_group(0, g)

            def m_rows(f, g, qc):
                sp.wait_ge(m_copied, f + 1)
                sp.dma_start(m_scratch[f].rearrange("s j (k q) -> (s j k) q", q=P), mt[:]).then_inc(m_written, 16)
                sp.wait_ge(m_written, 16 * (f + 1))
                sp.dma_start(Qs[g][STACK:ROWS, :, qc * CH:(qc + 1) * CH], m_scratch[f]).then_inc(m_loaded, 16)

            def sums(scratch, b):
                return scratch[b].rearrange("h c (s q) -> (h c s) q", q=SQ)

            def r_write(b):
                sp.dma_start(sums(r_scratch, b), s_c[:, b, :]).then_inc(r_written, 16)

            def o_write(G, b, g, qc):
                sp.wait_ge(o_copied, 2 * G + qc + 1)
                for j in range(HG):
                    rows = slice((g * HG + j) * D, (g * HG + j + 1) * D)
                    sp.dma_start(o_scratch[b * QC + qc, rows, :], ot[32 * j:32 * j + D, :]).then_inc(o_written, 16)
                sp.dma_start(s_scratch[b, g * HG:(g + 1) * HG, qc, :], ot[D:P:2 * D, :]).then_inc(o_written, 16)

            m_rows(0, 0, 0)

            def phase_b(b, last):
                for g in range(NG):
                    G = b * NG + g
                    if not last or g == 0:
                        sp.wait_ge(pv_done, UNITS * G)
                        load_group(b + (g + 3) // NG, (g + 3) % NG)
                    if last and g == 0:
                        sp.wait_ge(o_written, O_WRITES * 2 * NG * (B - 1))
                        for i in range(B - 1):
                            sp.dma_start(s_c[:, i, :], sums(s_scratch, i)).then_inc(s_loaded, 16)
                    m_rows(2 * G + 1, g, 1)
                    o_write(G, b, g, 0)
                    if not (last and g == NG - 1):
                        m_rows(2 * G + 2, (g + 1) % NG, 0)
                    o_write(G, b, g, 1)

            phase_b(0, False)
            with sp.Fori(1, B - 1) as b:
                phase_b(b, False)
            phase_b(B - 1, True)

            def load_o(b, qc):
                sp.dma_start(on_raw[:], o_scratch[b * QC + qc].rearrange("(k p) t -> p k t", p=P)).then_inc(on_loaded, 16)
                for k in range(KT):
                    sp.dma_start(r_raw[:, k, :], r_scratch[b, k * 8:(k + 1) * 8, qc, None, :].broadcast_to([8, D, CH])
                                 ).then_inc(on_loaded, 16)

            def load_xc(c):
                sp.dma_start(x_in[:], x_v[c]).then_inc(xc_loaded, 16)

            sp.wait_ge(recip_done, 1)
            for i in range(B - 1):
                r_write(i)
            sp.wait_ge(r_written, 16 * (B - 1))
            sp.wait_ge(prep_done, PREP_STEPS)
            sp.wait_ge(o_written, O_WRITES * 2 * GROUPS)
            load_o(0, 0)
            load_xc(0)
            sp.dma_start(s_c[:, B - 1, :], sums(s_scratch, B - 1)).then_inc(s_loaded, 16)

            def write_out(c):
                sp.wait_ge(out_added, 2 * c + 2)
                sp.dma_start(out_v[c], xo[:]).then_inc(out_written, 16)

            def phase_c(c, b, qc, first=False, last=False):
                if not last:
                    sp.wait_ge(o_normed, c + 1)
                    load_o(b, qc)
                    sp.wait_ge(xb_ready, c + 1)
                    load_xc(c + 1)
                if not first:
                    write_out(c - 1)

            phase_c(0, 0, 1, first=True)
            sp.wait_ge(recip_done, 2)
            r_write(B - 1)
            sp.wait_ge(r_written, 16 * B)
            with sp.Fori(1, B) as b:
                phase_c(2 * b - 1, b, 0)
                phase_c(2 * b, b, 1)
            phase_c(NCH - 1, None, None, last=True)
            write_out(NCH - 1)
            sp.wait_ge(out_written, 16 * NCH)

        @block.gpsimd
        def _(pool):
            pool.dma_start(xa[:], x_v[0]).then_inc(x_loaded, 16)
            pool.memset(ones[:], 1.0).then_inc(const_set, 1)
            pool.memset(mhalf[:], -0.5).then_inc(const_set, 1)
            pool.memset(eps[:], LN_EPS).then_inc(const_set, 1)
            pool.memset(msp[:], 0.0).then_inc(const_set, 1)
            pool.wait_ge(const_set, 4)
            def make_rstd(n, par=0):
                pool.wait_ge(mv_ready, n + 1)
                pool.tensor_tensor(veps[:, par], mv[:, par, :, 1], eps[:], ALU.add).then_inc(veps_done, 1)
                pool.wait_ge(veps_done, n + 1)
                pool.tensor_tensor(rstd[:, par], veps[:, par], mhalf[:], ALU.pow).then_inc(rstd_ready, 1)

            def part3(c, m):
                pool.wait_ge(part2_done, 4 * c + m + 1)
                pool.tensor_tensor(parts[:, m, 2, :], rest[:, m % 2, :], parts[:, m, 1, :],
                                   ALU.subtract).then_inc(parts_ready, 1)

            def phase_a(c, last=False):
                part3(c, 0)
                if not last:
                    make_rstd(c + 1)
                part3(c, 1)
                if not last:
                    pool.wait_ge(xn_ready, c + 2)
                    if not (isinstance(c, int) and c == NCH - 2):
                        pool.dma_start(xa[:], x_v[c + 2]).then_inc(x_loaded, 16)
                part3(c, 2)
                part3(c, 3)

            make_rstd(0)
            pool.wait_ge(xn_ready, 1)
            pool.dma_start(xa[:], x_v[1]).then_inc(x_loaded, 16)
            for g in range(NG):
                pool.wait_ge(const_set, 4 + g)
                pool.memset(Ks[g][STACK:ROWS, :, :], 1.0).then_inc(const_set, 1)
            pool.wait_ge(const_set, 4 + NG)
            phase_a(0)
            with pool.Fori(1, NCH - 2) as c:
                phase_a(c)
            phase_a(NCH - 2)
            phase_a(NCH - 1, True)

            def f_rstd(c, blk):
                n = BLK * c + blk
                s = blk % 2
                pool.wait_ge(fmv_ready, n + 1)
                pool.tensor_tensor(fveps[:, s:s + 1], fmv[:, s, 1:2], eps[:, 0:1], ALU.add).then_inc(fveps_done, 1)
                pool.wait_ge(fveps_done, n + 1)
                pool.tensor_tensor(frstd[:, s:s + 1], fveps[:, s:s + 1], mhalf[:, 0:1], ALU.pow).then_inc(frstd_ready, 1)

            def x_plus_b(c):
                pool.wait_ge(xc_loaded, 16 * (c + 1))
                pool.tensor_tensor(x_b[:], x_in[:], b_out[:, None, :].broadcast_to([P, BLK, E]),
                                   ALU.add).then_inc(xb_ready, 1)

            def normalise(c):
                pool.wait_ge(on_loaded, 16 * (1 + KT) * (c + 1))
                pool.tensor_tensor(onT[:], on_raw[:], r_raw[:], ALU.mult).then_inc(o_normed, 1)

            def keys_and_values(c, b):
                pool.tensor_copy(kcur[:], kbd[:, b]).then_inc(kv_copied, 1)
                pool.tensor_copy(vcur[:], vbd[:, b]).then_inc(kv_copied, 1)

            def x1_plus_b(c):
                for k in range(2):
                    pool.wait_ge(x_free[X_OUT[k] % 4], x1_count(c, k))
                pool.tensor_tensor(x1_b[:], x1[:], b_o2[:, None, :].broadcast_to([P, BLK, E]),
                                   ALU.add).then_inc(x1b_ready, 1)

            def x2_plus_b(c):
                pool.wait_ge(out_added, 2 * c)
                for i in (X_O2, X_O2 + 1):
                    pool.wait_ge(x_free[i % 4], free_count(c, i) + 1)
                pool.tensor_tensor(x2_f[:], x2[:], b_f[:, None, :].broadcast_to([P, BLK, E]),
                                   ALU.add).then_inc(x2_kept, 1)

            pool.wait_ge(c_weights, C_LOADS)
            pool.wait_ge(prep_done, PREP_STEPS)
            normalise(0)
            x_plus_b(0)
            keys_and_values(0, 0)
            make_rstd(NCH)

            def phase_c(c, b, first=False, last=False):
                x1_plus_b(c)
                if not first:
                    for blk in range(BLK):
                        f_rstd(c - 1, blk)
                if not last:
                    x_plus_b(c + 1)
                    pool.wait_ge(x_done, done_count(c, X_PV[1] + 1))
                    normalise(c + 1)
                    keys_and_values(c + 1, b)
                make_rstd(NCH + 2 * c + 1, 1)
                if not last:
                    make_rstd(NCH + 2 * c + 2)
                x2_plus_b(c)

            phase_c(0, 0, first=True)
            with pool.Fori(1, B) as b:
                phase_c(2 * b - 1, b)
                phase_c(2 * b, b)
            phase_c(NCH - 1, None, last=True)
            for blk in range(BLK):
                f_rstd(NCH - 1, blk)

        @block.scalar
        def _(act):
            for h in range(2):
                for k in range(KT):
                    act.dma_start(ctx_dup[:, k, :, h, :],
                                  ctxT[k * P:(k + 1) * P, :].rearrange("p (b t) -> p b t", b=B)).then_inc(c_weights, 16)
            for t, d in ((w_out, wout), (w_q2, wqT), (w_k2, wkT), (w_v2, wvT), (w_o2, woT), (w_fc, wfcT), (w_p, wpT)):
                act.dma_start(t[:], d.rearrange("(k p) n -> p k n", p=P)).then_inc(c_weights, 16)
            for t, d in ((b_q2, bq2), (b_k2, bk2), (ln_w, lnw), (ln_b, lnb), (head_mask, head_mask_in),
                         (half_mask, half_mask_in), (ones_bd, ones_bd_in), (b_out, bout.partition_broadcast(P)),
                         (b_v2, bv2.partition_broadcast(P)), (b_o2, bo2.partition_broadcast(P))):
                act.dma_start(t[:], d).then_inc(c_weights, 16)
            act.wait_ge(a_weights, 16 * 4)
            act.activation(ident_b[:], ident[:], ACT.Copy).then_inc(ident_b_set, 1)

            def xT_copy(c, par):
                for k in range(KT):
                    act.wait_ge(tr_done, 2 * c + k + 1)
                    act.activation(xnT_a[:, par, k, :], ps[:, k, :], ACT.Copy).then_inc(xT_copied, 1)

            def part1(c, m):
                act.wait_ge(qk_mm_done, 4 * c + m + 1)
                if m == 0:
                    act.wait_ge(parts_written, 16 * 4 * c)
                act.activation(parts[:, m, 0, :], ps[:, 4 + m, :], ACT.Identity,
                               bias=b_qk[:, m:m + 1]).then_inc(part1_done, 1)

            def part2(c, m):
                act.wait_ge(rest_done, 4 * c + m + 1)
                act.activation(parts[:, m, 1, :], rest[:, m % 2, :], ACT.Copy).then_inc(part2_done, 1)

            def phase_a(c, par, last=False):
                part1(c, 0)
                part1(c, 1)
                part2(c, 0)
                part1(c, 2)
                part2(c, 1)
                if not last:
                    xT_copy(c + 1, 1 - par)
                part2(c, 2)
                part1(c, 3)
                part2(c, 3)

            xT_copy(0, 0)
            phase_a(0, 0)
            with act.Fori(1, NCH - 1, 2) as c:
                phase_a(c, 1)
                phase_a(c + 1, 0)
            phase_a(NCH - 1, 1, True)

            junk = vx[:].rearrange("p b h d -> p (b h d)")
            act.wait_ge(v_written, 16 * NG * NCH)
            act.wait_ge(c_weights, C_LOADS)
            for i, w in enumerate((w_fc, w_p)):
                act.wait_ge(abs_summed, i)
                act.activation(junk, w[:].rearrange("p k n -> p (k n)"), ACT.Abs,
                               accum_out=abs_sum[:, i:i + 1]).then_inc(abs_summed, 1)

            def m_copy(f, qc):
                act.wait_ge(m_transposed, f + 1)
                act.wait_ge(m_written, 16 * f)
                act.activation(mt[:], ps[:, 5 + M_SLOTS[qc] % 3, :].bitcast(BF16)[0:48, 0:P], ACT.Copy).then_inc(m_copied, 1)

            def exps(U, par):
                for h in range(2):
                    act.wait_ge(st_done, 2 * U + h + 1)
                    act.activation(prob[:, par, h].rearrange("p a q -> p (a q)"),
                                   ps[:, 2 * h:2 * h + 2, :].rearrange("p a q -> p (a q)"),
                                   ACT.Exp).then_inc(exp_done, 1)

            act.wait_ge(abs_summed, 2)
            m_copy(0, 0)
            exps(0, 0)

            def phase_b(b, last):
                for g in range(NG):
                    G = b * NG + g
                    end = last and g == NG - 1
                    for s in range(UNITS):
                        U = G * UNITS + s
                        if s == 3:
                            m_copy(2 * G + 1, 1)
                        if s == 11 and not end:
                            m_copy(2 * G + 2, 0)
                        if not (end and s == UNITS - 1):
                            act.wait_ge(pv_done, U)
                            exps(U + 1, (s + 1) % 2)
                        if s % KB == KB - 1:
                            qc = s // KB
                            act.wait_ge(pv_done, U + 1)
                            act.wait_ge(o_written, O_WRITES * (2 * G + qc))
                            act.activation(ot[:], ps[:, 4, :], ACT.Copy).then_inc(o_copied, 1)

            phase_b(0, False)
            with act.Fori(1, B - 1) as b:
                phase_b(b, False)
            phase_b(B - 1, True)

            def x_ready(c, i):
                act.wait_ge(x_done, done_count(c, i))

            def x_copy(c, i, dst, done=None):
                x_ready(c, i)
                act.activation(dst, ps[:, i % 4, :], ACT.Copy).then_inc(done or x_free[i % 4], 1)

            def gelu(c, blk):
                act.wait_ge(fc_done, BLK * c + blk + 1)
                act.wait_ge(xhat_done, BLK * c + max(blk - 1, 0))
                r = 4 + 2 * (blk % 2)
                act.activation(gl[:, blk % 2, :], ps[:, r:r + 2, :].rearrange("p a q -> p (a q)"),
                               ACT.Gelu).then_inc(gelu_done, 1)

            def ft_high(c, t):
                act.wait_ge(hT_done, HT * c + t + 1)
                act.activation(fT[:, t % 2, 0, :].bitcast(F32R), ps[:, 4 + t % 2, :], ACT.Identity,
                               scale=ln_w[:, t:t + 1]).then_inc(fh_ready, 1)

            def c_exp(c, m, blk):
                act.wait_ge(sc_ready, 8 * c + 4 * m + blk + 1)
                act.activation(pe_[:, blk, :], sc[:, blk % 2, :], ACT.Exp, scale=0.25).then_inc(p_ready, 1)

            def phase_c(c, first, last):
                def ffn(f, *a):
                    if not first:
                        f(c - 1, *a)
                ffn(gelu, 0)
                ffn(gelu, 1)
                for k in range(KT):
                    x_copy(c, X_T2 + k, xn2T[:, k, :])
                ffn(gelu, 2)
                for m in range(KT):
                    x_ready(c, X_Q2 + m)
                    act.activation(q2T[:, m, :], ps[:, (X_Q2 + m) % 4, :], ACT.Identity,
                                   bias=b_q2[:, m:m + 1]).then_inc(x_free[(X_Q2 + m) % 4], 1)
                ffn(gelu, 3)
                for m in range(KT):
                    for blk in range(BLK):
                        c_exp(c, m, blk)
                        if m == 1 and blk % 2 == 1:
                            ffn(ft_high, 2 + blk // 2)
                    if m == 0:
                        ffn(ft_high, 0)
                    for blk in range(BLK):
                        i = X_PT[m] + blk
                        x_ready(c, i)
                        act.activation(pT[:, m, :, blk * P:(blk + 1) * P],
                                       ps[:, i % 4, :].rearrange("p (r q) -> p r q", r=4),
                                       ACT.Copy).then_inc(x_free[i % 4], 1)
                    ffn(ft_high, 1 if m == 0 else 4)
                for t in range(5, HT):
                    ffn(ft_high, t)
                for k in range(KT):
                    x_copy(c, X_T3 + k, xn3T[:, 0, k, :].bitcast(F32R), xh_high)

            phase_c(0, True, False)
            phase_c(1, False, False)
            with act.Fori(2, NCH - 1) as c:
                phase_c(c, False, False)
            phase_c(NCH - 1, False, True)
            for blk in range(BLK):
                gelu(NCH - 1, blk)
            for t in range(HT):
                ft_high(NCH - 1, t)

        @block.vector
        def _(dve):
            dve.memset(vx[:, :, :, D:32], float(E) ** 0.5).then_inc(ones_set, 1)

            def ln_stats(n, src, par=0):
                for blk in range(BLK):
                    i = dve.bn_stats(stats[:, par, blk, :], src[:, blk, :])
                i.then_inc(stats_done, 1)
                dve.wait_ge(stats_done, n + 1)
                dve.tensor_copy(touch[:], stats[:, par, 0, 0:1])
                for blk in range(BLK):
                    i = dve.bn_aggr(mv[:, par, blk, :], stats[:, par, blk, :])
                i.then_inc(mv_ready, 1)

            def ln_apply(n, src, dst, par=0):
                dve.wait_ge(rstd_ready, n + 1)
                for blk in range(BLK):
                    i = dve.tensor_scalar(dst[:, blk, :], src[:, blk, :], mv[:, par, blk, 0:1], rstd[:, par, blk:blk + 1],
                                          ALU.subtract, ALU.mult)
                i.then_inc(xn_ready, 1)

            def a_stats(c):
                dve.wait_ge(x_loaded, 16 * (c + 1))
                ln_stats(c, xa)

            def a_apply(c):
                dve.wait_ge(tr_done, 2 * c)
                ln_apply(c, xa, xn_a)

            def v_copy(c):
                dve.wait_ge(v_written, 16 * NG * c)
                for i in range(2):
                    dve.wait_ge(v_mm_done, 2 * c + i + 1)
                    dve.tensor_tensor(vx[:, 2 * i:2 * i + 2, :, 0:D],
                                      ps[:, 2 + i, :].rearrange("p (b h d) -> p b h d", b=2, h=H),
                                      b_v[:].rearrange("p (b h d) -> p b h d", b=1, h=H).broadcast_to([P, 2, H, D]),
                                      ALU.add).then_inc(v_copied, 1)

            def rest1(c, m):
                dve.wait_ge(parts_ready, 4 * c + max(m - 1, 0))
                dve.wait_ge(part1_done, 4 * c + m + 1)
                dve.scalar_tensor_tensor(out=rest[:, m % 2, :], in0=ps[:, 4 + m, :], scalar=b_qk[:, m:m + 1],
                                         in1=parts[:, m, 0, :], op0=ALU.add, op1=ALU.subtract).then_inc(rest_done, 1)

            def phase_a(c, last):
                v_copy(c)
                rest1(c, 0)
                if not last:
                    a_stats(c + 1)
                rest1(c, 1)
                if not last:
                    a_apply(c + 1)
                rest1(c, 2)
                rest1(c, 3)

            a_stats(0)
            a_apply(0)
            dve.wait_ge(a_weights, 16 * 4)
            dve.wait_ge(ones_set, 1)
            phase_a(0, False)
            with dve.Fori(1, NCH - 1) as c:
                phase_a(c, False)
            phase_a(NCH - 1, True)

            def reduce_tile(G, t):
                dve.wait_ge(max_mm_done, MAXT * G + t + 1)
                qc, i = divmod(t, MAXT // 2)
                dve.tensor_reduce(maxes[:, qc, i // 2, i % 2:i % 2 + 1], ps[:, 5 + max_slot(t) % 3, :], AX.X,
                                  ALU.max).then_inc(max_reduced, 1)

            def split_max(f, qc, step):
                if step == 0:
                    dve.wait_ge(max_reduced, (MAXT // 2) * (f + 1))
                    dve.tensor_tensor(mrow[:], maxes[:, qc, :, 0], maxes[:, qc, :, 1], ALU.max).then_inc(m_step, 1)
                elif step == 1:
                    dve.wait_ge(m_step, 3 * f + 1)
                    dve.wait_ge(m_transposed, f)
                    dve.tensor_scalar(msp[:, 0, :], mrow[:], -1.0, None, ALU.mult).then_inc(m_step, 1)
                elif step == 2:
                    dve.wait_ge(m_step, 3 * f + 2)
                    dve.scalar_tensor_tensor(out=mrest[:], in0=mrow[:], scalar=-1.0, in1=msp[:, 0, :],
                                             op0=ALU.mult, op1=ALU.subtract).then_inc(m_step, 1)
                elif step == 3:
                    dve.wait_ge(m_step, 3 * f + 3)
                    dve.tensor_copy(msp[:, 1, :], mrest[:]).then_inc(m_split, 1)
                else:
                    dve.wait_ge(m_split, 2 * f + 1)
                    dve.tensor_tensor(msp[:, 2, :], mrest[:], msp[:, 1, :], ALU.subtract).then_inc(m_split, 1)

            def max_pass(G, splits=True):
                for t in range(MAXT):
                    reduce_tile(G, t)
                    if t % (MAXT // 2) < 5:
                        if t >= MAXT // 2:
                            split_max(2 * G, 0, t - MAXT // 2)
                        elif splits:
                            split_max(2 * G - 1, 1, t)

            max_pass(0, False)

            def phase_b(b, last):
                for g in range(NG - 1 if last else NG):
                    max_pass(b * NG + g + 1)

            phase_b(0, False)
            with dve.Fori(1, B - 1) as b:
                phase_b(b, False)
            phase_b(B - 1, True)
            for step in range(5):
                split_max(2 * GROUPS - 1, 1, step)

            def reciprocals(n, lo, hi):
                dve.wait_ge(s_loaded, 16 * hi)
                dve.reciprocal(s_c[:, lo:hi, :], s_c[:, lo:hi, :]).then_inc(recip_done, 1)

            reciprocals(0, 0, B - 1)

            dve.wait_ge(c_weights, C_LOADS)
            n = 0
            dve.wait_ge(prep_mm, 1)
            for m in range(KT):
                src = ps[:, 5, m * B * CTX:(m + 1) * B * CTX].rearrange("p (b t) -> p b t", b=B)
                for h in range(8):
                    i = dve.tensor_scalar(kbd[:, :, (m * 8 + h) * CTX:(m * 8 + h + 1) * CTX], src, b_k2[:, m:m + 1], head_mask[:, h:h + 1],
                                          ALU.add, ALU.mult)
            i.then_inc(prep_done, 1)
            n += 1
            for b in range(B):
                dve.wait_ge(prep_mm, 2 + b // 2)
                dve.tensor_tensor(v2b[:], ps[:, 6 + b // 2, (b % 2) * E:(b % 2 + 1) * E], b_v2[:],
                                  ALU.add).then_inc(prep_done, 1)
                n += 1
                dve.wait_ge(prep_done, n)
                v2v = v2b[:].rearrange("p (r h d) -> p r h d", r=PAIRS, h=2)
                for h in range(2):
                    i = dve.tensor_scalar(vbd[:, b].rearrange("p (r h d) -> p r h d", r=PAIRS, h=2)[:, :, h, :], v2v[:, :, h, :], half_mask[:, h:h + 1], None, ALU.mult)
                i.then_inc(prep_done, 1)
                n += 1
                dve.wait_ge(prep_done, n)
            dve.wait_ge(prep_mm, 4)
            dve.tensor_scalar(thr[:, 0, :], ps[:, 5, 0:2], 1.0 / (E * F), ABS_EPS, ALU.mult, ALU.add).then_inc(prep_done, 1)
            n += 1
            dve.wait_ge(prep_done, n)
            dve.tensor_scalar(thr[:, 1, :], thr[:, 0, :], 0.5, None, ALU.mult)
            dve.tensor_scalar(thr[:, 2, :], thr[:, 0, :], -0.5, None, ALU.mult).then_inc(prep_done, 1)
            n += 1
            dve.wait_ge(prep_done, n)
            neg = vx[:].rearrange("p b h d -> p (b h d)")
            for i, (w, ternary) in enumerate(((w_fc, t_fc), (w_p, t_p))):
                wf = w[:].rearrange("p k n -> p (k n)")
                dve.tensor_scalar(neg, wf, thr[:, 2, i:i + 1], None, ALU.is_lt).then_inc(prep_done, 1)
                n += 1
                dve.wait_ge(prep_done, n)
                dve.scalar_tensor_tensor(out=ternary[:].rearrange("p k n -> p (k n)").bitcast(F32R), in0=wf,
                                         scalar=thr[:, 1, i:i + 1], in1=neg,
                                         op0=ALU.is_gt, op1=ALU.subtract).then_inc(prep_done, 1)
                n += 1
                dve.wait_ge(prep_done, n)
            dve.tensor_tensor(vx[:, 0:2].rearrange("p b h d -> p (b h d)").rearrange("p (t c) -> p t c", t=HT),
                              ln_b[:, :, None].broadcast_to([P, HT, P]),
                              ones[:, None, :].broadcast_to([P, HT, P]), ALU.mult).then_inc(prep_done, 1)
            n += 1
            dve.wait_ge(prep_mm, 5)
            dve.tensor_copy(b_f[:], ps[:, 6, 0:E]).then_inc(prep_done, 1)
            n += 1
            assert n == PREP_STEPS

            def x_ready(c, i):
                dve.wait_ge(x_done, done_count(c, i))

            def add_tile(c, i, dst, src, k):
                x_ready(c, i)
                dve.tensor_tensor(dst[:, 2 * k:2 * k + 2, :], ps[:, i % 4, :].rearrange("p (b e) -> p b e", b=2),
                                  src[:, 2 * k:2 * k + 2, :], ALU.add).then_inc(x_free[i % 4], 1)

            def scores(c, m, blk, first):
                i = X_S[m] + blk
                s = ps[:, i % 4, :].rearrange("p (h t) -> p h t", h=8)
                x_ready(c, i)
                k = blk % 2
                if not first or 4 * m + blk >= 2:
                    dve.wait_ge(p_ready, 8 * c + 4 * m + blk - 1)
                dve.tensor_reduce(nmx[:, k, :], s, AX.X, ALU.max, negate=True).then_inc(nmx_done, 1)
                dve.wait_ge(nmx_done, 8 * c + 4 * m + blk + 1)
                dve.tensor_tensor(sc[:, k, :].rearrange("p (h t) -> p h t", h=8), s,
                                  nmx[:, k, :, None].broadcast_to([P, 8, CTX]), ALU.add).then_inc(sc_ready, 1)

            def x_norm(c, m):
                i = X_PV[m]
                x_ready(c, i + 1)
                if m == 1:
                    dve.wait_ge(x_free[X_PV[0] % 4], free_count(c, X_PV[0]) + 1)
                dve.reciprocal(rs2[:], ps[:, (i + 1) % 4, :]).then_inc(x_free[(i + 1) % 4], 1)
                dve.wait_ge(x_free[(i + 1) % 4], free_count(c, i + 1) + 1)
                dve.tensor_tensor(o2T[:, m, :], ps[:, i % 4, :], rs2[:], ALU.mult).then_inc(x_free[i % 4], 1)

            def f_stats(c, blk):
                n = BLK * c + blk
                k = blk % 2
                dve.wait_ge(gelu_done, n + 1)
                for h in range(2):
                    i = dve.bn_stats(fstats[:, k, h, :], gl[:, k, h * 512:(h + 1) * 512])
                i.then_inc(fstats_done, 1)
                dve.wait_ge(fstats_done, n + 1)
                dve.tensor_copy(touch[:], fstats[:, k, 0, 0:1])
                dve.bn_aggr(fmv[:, k, :], fstats[:, k, :, :]).then_inc(fmv_ready, 1)

            def f_apply(c, blk):
                k = blk % 2
                dve.wait_ge(frstd_ready, BLK * c + blk + 1)
                dve.tensor_scalar(xhat[:, blk, :], gl[:, k, :], fmv[:, k, 0:1], frstd[:, k:k + 1],
                                  ALU.subtract, ALU.mult).then_inc(xhat_done, 1)

            def x1_half(c, k):
                r = X_OUT[k] % 4
                dve.wait_ge(x_done, (k + 1) if isinstance(c, int) and c == 0 else done_count(c - 1, X_OUT[k]))
                dve.tensor_tensor(x1[:, 2 * k:2 * k + 2, :], ps[:, r, :].rearrange("p (b e) -> p b e", b=2),
                                  x_b[:, 2 * k:2 * k + 2, :], ALU.add).then_inc(x_free[r], 1)

            def x1_stats(c):
                for k in range(2):
                    dve.wait_ge(x_free[X_OUT[k] % 4], x1_count(c, k))
                ln_stats(NCH + 2 * c, x1)

            def ft_low(c, t):
                dve.wait_ge(fh_ready, HT * c + t + 1)
                dve.scalar_tensor_tensor(out=fT[:, t % 2, 1, :].bitcast(F32R), in0=ps[:, 4 + t % 2, :],
                                         scalar=ln_w[:, t:t + 1], in1=fT[:, t % 2, 0, :],
                                         op0=ALU.mult, op1=ALU.subtract).then_inc(ft_ready, 1)

            def x3_low(c):
                for k in range(KT):
                    i = X_T3 + k
                    dve.wait_ge(xh_high, KT * c + k + 1)
                    dve.tensor_tensor(xn3T[:, 1, k, :].bitcast(F32R), ps[:, i % 4, :], xn3T[:, 0, k, :],
                                      ALU.subtract).then_inc(x_free[i % 4], 1)

            def f_out(c):
                dve.wait_ge(acc_done, c + 1)
                dve.wait_ge(x2_kept, c + 1)
                dve.wait_ge(out_written, 16 * c)
                for i in range(2):
                    dve.tensor_tensor(xo[:, 2 * i:2 * i + 2, :], ps[:, 6 + i, :].rearrange("p (b e) -> p b e", b=2),
                                      x2_f[:, 2 * i:2 * i + 2, :], ALU.add).then_inc(out_added, 1)

            dve.wait_ge(xb_ready, 1)
            for k in range(2):
                x1_half(0, k)
            x1_stats(0)
            ln_apply(NCH, x1, xn_1)

            def phase_c(c, first, last):
                def ffn(f, *a):
                    if not first:
                        f(c - 1, *a)
                ffn(f_stats, 0)
                ffn(f_stats, 1)
                ffn(f_apply, 0)
                ffn(f_stats, 2)
                ffn(f_apply, 1)
                ffn(f_stats, 3)
                ffn(f_apply, 2)
                scores(c, 0, 0, first)
                ffn(f_apply, 3)
                for blk in range(1, BLK):
                    scores(c, 0, blk, first)
                ffn(ft_low, 0)
                if first:
                    reciprocals(1, B - 1, B)
                scores(c, 1, 0, first)
                ffn(ft_low, 1)
                for blk in range(1, BLK):
                    scores(c, 1, blk, first)
                    if blk >= 2:
                        ffn(ft_low, blk)
                x_norm(c, 0)
                ffn(ft_low, 4)
                x_norm(c, 1)
                for t in range(5, HT):
                    ffn(ft_low, t)
                dve.wait_ge(x1b_ready, c + 1)
                if not first:
                    dve.wait_ge(x2_kept, c)
                for k in range(2):
                    add_tile(c, X_O2 + k, x2, x1_b, k)
                for i in (X_O2, X_O2 + 1):
                    dve.wait_ge(x_free[i % 4], free_count(c, i) + 1)
                ln_stats(NCH + 2 * c + 1, x2, 1)
                ffn(f_out)
                ln_apply(NCH + 2 * c + 1, x2, xn_2, 1)
                if not last:
                    dve.wait_ge(xb_ready, c + 2)
                    x1_half(c + 1, 0)
                x3_low(c)
                if not last:
                    x1_half(c + 1, 1)
                    x1_stats(c + 1)
                    ln_apply(NCH + 2 * c + 2, x1, xn_1)

            phase_c(0, True, False)
            phase_c(1, False, False)
            with dve.Fori(2, NCH - 1) as c:
                phase_c(c, False, False)
            phase_c(NCH - 1, False, True)
            for blk in range(BLK):
                f_stats(NCH - 1, blk)
                f_apply(NCH - 1, blk)
            for t in range(HT):
                ft_low(NCH - 1, t)
            f_out(NCH - 1)

        @block.tensor
        def _(pe):
            def mm(o, lhsT, rhs, k, n, **kw):
                return pe.matmul(o, lhsT, rhs, start=(k == 0), stop=(k == n - 1), **kw)

            def a_transpose(c):
                pe.wait_ge(xn_ready, c + 1)
                pe.wait_ge(xT_copied, 2 * c)
                for k in range(KT):
                    for blk in range(BLK):
                        i = pe.transpose(ps[:, k, blk * P:(blk + 1) * P], xn_a[:, blk, k * P:(k + 1) * P], ident[:])
                    i.then_inc(tr_done, 1)

            def a_v(c, par):
                pe.wait_ge(xT_copied, 2 * c + 2)
                pe.wait_ge(v_copied, 2 * c)
                for blk in range(BLK):
                    for k in range(KT):
                        i = mm(ps[:, 2 + blk // 2, (blk % 2) * E:(blk % 2 + 1) * E],
                               xnT_a[:, par, k, blk * P:(blk + 1) * P], w_qkv[:, k, 2 * E:3 * E], k, KT)
                    if blk % 2:
                        i.then_inc(v_mm_done, 1)

            def a_qk(c, m, par):
                if m == 0:
                    pe.wait_ge(rest_done, 4 * c)
                for k in range(KT):
                    i = mm(ps[:, 4 + m, :], w_qkv[:, k, m * P:(m + 1) * P], xnT_a[:, par, k, :], k, KT)
                i.then_inc(qk_mm_done, 1)

            def phase_a(c, par, last=False):
                a_v(c, par)
                for m in range(3):
                    a_qk(c, m, par)
                if not last:
                    a_transpose(c + 1)
                a_qk(c, 3, par)

            pe.wait_ge(a_weights, 16 * 4)
            pe.wait_ge(const_set, 4)
            pe.wait_ge(ident_b_set, 1)
            a_transpose(0)
            phase_a(0, 0)
            with pe.Fori(1, NCH - 1, 2) as c:
                phase_a(c, 1)
                phase_a(c + 1, 0)
            phase_a(NCH - 1, 1, True)

            def prepare(n):
                if n == 0:
                    pe.wait_ge(c_weights, C_LOADS)
                    pe.wait_ge(max_reduced, MAXT * GROUPS)
                    pe.wait_ge(m_copied, 2 * GROUPS)
                    for m in range(KT):
                        for k in range(KT):
                            i = mm(ps[:, 5, m * B * CTX:(m + 1) * B * CTX].rearrange("p (b t) -> p b t", b=B),
                                   w_k2[:, k, m * P:(m + 1) * P], ctx_dup[:, k, :, 0, :], k, KT)
                elif n <= 2:
                    for b in (2 * n - 2, 2 * n - 1):
                        for k in range(KT):
                            i = mm(ps[:, 5 + n, (b % 2) * E:(b % 2 + 1) * E],
                                   ctx_dup[:, k, b, :, :].rearrange("p c t -> p (c t)"), w_v2[:, k, :], k, KT)
                elif n == 4:
                    pe.wait_ge(prep_done, PREP_STEPS - 1)
                    lb = vx[:, 0:2].rearrange("p b h d -> p (b h d)")
                    for t in range(HT):
                        i = mm(ps[:, 6, 0:E], lb[:, t * P:(t + 1) * P], t_p[:, t, :], t, HT)
                else:
                    pe.wait_ge(abs_summed, 2)
                    pe.wait_ge(prep_done, 1)
                    i = pe.matmul(ps[:, 5, 0:2], ones[:], abs_sum[:], start=True, stop=True)
                i.then_inc(prep_mm, 1)

            pe.wait_ge(rest_done, 4 * NCH)

            def slot_free(G, k, first):
                k -= 3
                if k in M_SLOTS:
                    f = 2 * G + (0 if k == M_SLOTS[0] else -1)
                    if not (first and k == M_SLOTS[1]):
                        pe.wait_ge(m_copied, f + 1)
                elif k >= 0:
                    t = [max_slot(t) for t in range(MAXT)].index(k)
                    pe.wait_ge(max_reduced, MAXT * G + t + 1)
                elif not first:
                    pe.wait_ge(max_reduced, MAXT * G + k + 1)

            def max_tile(G, g, t, first=False):
                qc, i = divmod(t, MAXT // 2)
                j, blk, half = i // 8, (i % 8) // 2, i % 2
                q0 = qc * CH + blk * P
                slot_free(G, max_slot(t), first)
                pe.matmul(ps[:, 5 + max_slot(t) % 3, :], Qs[g][0:STACK, j, q0:q0 + P],
                          Ks[g][0:STACK, j, half * 512:(half + 1) * 512], start=True, stop=True).then_inc(max_mm_done, 1)

            def max_transpose(G, f, qc, last=False):
                k = M_SLOTS[qc]
                if last:
                    pe.wait_ge(max_reduced, MAXT * GROUPS)
                else:
                    slot_free(G, k, False)
                pe.wait_ge(m_split, 2 * f + 2)
                pe.transpose(ps[:, 5 + k % 3, :].bitcast(BF16)[0:96, 0:P], msp[:].rearrange("p s i -> p (s i)"),
                             ident_b[:]).then_inc(m_transposed, 1)

            def scores(U, g, s, h, free=True):
                qc, kb = divmod(s, KB)
                if free:
                    pe.wait_ge(exp_done, 2 * U + h - 1)
                for j in (2 * h, 2 * h + 1):
                    i = pe.matmul(ps[:, j, :], Ks[g][0:ROWS, j, kb * P:(kb + 1) * P],
                                  Qs[g][0:ROWS, j, qc * CH:(qc + 1) * CH], start=True, stop=True)
                i.then_inc(st_done, 1)

            def values(G, g, U, s):
                qc, kb = divmod(s, KB)
                pe.wait_ge(exp_done, 2 * U + 2)
                if kb == 0:
                    pe.wait_ge(o_copied, 2 * G + qc)
                for j in range(HG):
                    i = pe.matmul(ps[32 * j:32 * j + 32, 4, :], Vs[g][:, kb, 32 * j:32 * j + 32],
                                  prob[:, s % 2, j // 2, j % 2, :], start=(kb == 0), stop=(kb == KB - 1))
                i.then_inc(pv_done, 1)

            pe.wait_ge(group_loaded[0], GROUP_LOADS)
            pe.wait_ge(const_set, 4 + NG)
            for t in range(MAXT):
                if t == 40:
                    max_transpose(0, 0, 0)
                max_tile(0, 0, t, True)
            pe.wait_ge(m_loaded, 16)
            scores(0, 0, 0, 0, False)
            scores(0, 0, 0, 1, False)

            def phase_b(b, last):
                for g in range(NG):
                    G = b * NG + g
                    end = last and g == NG - 1
                    g1 = (g + 1) % NG
                    for s in range(UNITS):
                        U = G * UNITS + s
                        if s == 0 and not end:
                            pe.wait_ge(group_loaded[g1], GROUP_LOADS * (b + (g + 1) // NG + 1))
                        if s == 2:
                            max_transpose(G + 1, 2 * G + 1, 1, end)
                        if s == 10 and not end:
                            max_transpose(G + 1, 2 * G + 2, 0)
                        if s == KB - 1:
                            pe.wait_ge(m_loaded, 16 * (2 * G + 2))
                        if s == UNITS - 1 and not end:
                            pe.wait_ge(m_loaded, 16 * (2 * G + 3))
                        for h in range(2):
                            if not end:
                                max_tile(G + 1, g1, 4 * s + h)
                            if not (end and s == UNITS - 1):
                                nxt = (g1, 0) if s == UNITS - 1 else (g, s + 1)
                                scores(U + 1, nxt[0], nxt[1], h)
                        if not end:
                            max_tile(G + 1, g1, 4 * s + 2)
                        values(G, g, U, s)
                        if end and s % 2 == 0 and 4 <= s < 12:
                            prepare(s // 2 - 2)
                        if not end:
                            max_tile(G + 1, g1, 4 * s + 3)

            phase_b(0, False)
            with pe.Fori(1, B - 1) as b:
                phase_b(b, False)
            phase_b(B - 1, True)

            pe.wait_ge(o_copied, 2 * GROUPS)
            pe.wait_ge(max_reduced, MAXT * GROUPS)
            pe.wait_ge(m_copied, 2 * GROUPS)
            prepare(4)

            def x_bank(c, i):
                before = i - 4
                if is_score(before):
                    m = 0 if before < X_S[1] else 1
                    pe.wait_ge(sc_ready, 8 * c + 4 * m + before - X_S[m] + 1)
                else:
                    pe.wait_ge(x_free[i % 4], free_count(c, i))
                return i % 4

            def pair_of_blocks(r, t, lhs, w):
                for h in range(2):
                    blk = 2 * t + h
                    for k in range(KT):
                        n = mm(ps[:, r, h * E:(h + 1) * E], lhs[:, k, blk * P:(blk + 1) * P], w[:, k, :], k, KT)
                n.then_inc(x_done, 1)

            def transposes(c, i, xn):
                for k in range(KT):
                    r = x_bank(c, i + k)
                    for blk in range(BLK):
                        n = pe.transpose(ps[:, r, blk * P:(blk + 1) * P], xn[:, blk, k * P:(k + 1) * P], ident[:])
                    n.then_inc(x_done, 1)

            def ready(c, i):
                pe.wait_ge(x_free[i % 4], free_count(c, i) + 1)

            def q2(c):
                for k in range(KT):
                    ready(c, X_T2 + k)
                for m in range(KT):
                    r = x_bank(c, X_Q2 + m)
                    for k in range(KT):
                        n = mm(ps[:, r, :], w_q2[:, k, m * P:(m + 1) * P], xn2T[:, k, :], k, KT)
                    n.then_inc(x_done, 1)

            def x_scores(c, m):
                if m == 0:
                    pe.wait_ge(kv_copied, 2 * c + 2)
                    ready(c, X_Q2)
                else:
                    ready(c, X_Q2 + 1)
                for blk in range(BLK):
                    r = x_bank(c, X_S[m] + blk)
                    pe.matmul(ps[:, r, :], q2T[:, m, blk * P:(blk + 1) * P], kcur[:, m * 8 * CTX:(m + 1) * 8 * CTX],
                              start=True, stop=True).then_inc(x_done, 1)

            def x_pT(c, m):
                for blk in range(BLK):
                    r = x_bank(c, X_PT[m] + blk)
                    pe.wait_ge(p_ready, 8 * c + 4 * m + blk + 1)
                    for pr in range(4):
                        n = pe.transpose(ps[:, r, pr * P:(pr + 1) * P], pe_[:, blk, pr * P:(pr + 1) * P], ident[:])
                    n.then_inc(x_done, 1)

            def x_values(c, m):
                for blk in range(BLK):
                    ready(c, X_PT[m] + blk)
                for t in range(2):
                    r = x_bank(c, X_PV[m] + t)
                    for pr in range(4):
                        n = pe.matmul(ps[32 * pr:32 * pr + 32, r, :], vcur[:, (4 * m + pr) * 32:(4 * m + pr + 1) * 32] if t == 0 else ones_bd[:],
                                      pT[:, m, pr, :], start=True, stop=True)
                    n.then_inc(x_done, 1)

            def fc(c, blk):
                if blk == 0:
                    for i in (X_T3, X_T3 + 1):
                        ready(c, i)
                    pe.wait_ge(ft_ready, HT * c)
                elif blk == 1:
                    pe.wait_ge(out_added, 2 * c)
                else:
                    pe.wait_ge(gelu_done, BLK * c + blk - 1)
                for h in range(2):
                    for n, (part, k) in enumerate((part, k) for part in range(2) for k in range(KT)):
                        i = mm(ps[:, 4 + 2 * (blk % 2) + h, :], xn3T[:, part, k, blk * P:(blk + 1) * P].bitcast(F32R),
                               t_fc[:, k, h * 512:(h + 1) * 512].bitcast(F32R), n, 2 * KT)
                i.then_inc(fc_done, 1)

            def f_tile(c, t):
                if t < HT:
                    if t == 0:
                        pe.wait_ge(xhat_done, BLK * (c + 1))
                    elif t >= 2:
                        pe.wait_ge(ft_ready, HT * c + t - 1)
                    for blk in range(BLK):
                        i = pe.transpose(ps[:, 4 + t % 2, blk * P:(blk + 1) * P], xhat[:, blk, t * P:(t + 1) * P], ident[:])
                    i.then_inc(hT_done, 1)
                if t >= 1:
                    pe.wait_ge(ft_ready, HT * c + t)
                    for blk in range(BLK):
                        for part in range(2):
                            i = pe.matmul(ps[:, 6 + blk // 2, (blk % 2) * E:(blk % 2 + 1) * E],
                                          fT[:, (t - 1) % 2, part, blk * P:(blk + 1) * P].bitcast(F32R),
                                          t_p[:, t - 1, :].bitcast(F32R),
                                          start=(t == 1 and blk % 2 == 0 and part == 0), stop=(t == HT and part == 1),
                                          skip_group_check=True)
                    if t == HT:
                        i.then_inc(acc_done, 1)

            def phase_c(c, first, last):
                def ffn(f, *a):
                    if not first:
                        f(c - 1, *a)
                ffn(fc, 0)
                ffn(fc, 1)
                pe.wait_ge(xn_ready, NCH + 2 * c + 1)
                transposes(c, X_T2, xn_1)
                ffn(fc, 2)
                q2(c)
                ffn(fc, 3)
                x_scores(c, 0)
                ffn(f_tile, 0)
                x_pT(c, 0)
                ffn(f_tile, 1)
                x_scores(c, 1)
                ffn(f_tile, 2)
                x_values(c, 0)
                ffn(f_tile, 3)
                x_pT(c, 1)
                ffn(f_tile, 4)
                x_values(c, 1)
                ffn(f_tile, 5)
                ffn(f_tile, 6)
                for m in range(KT):
                    ready(c, X_PV[m])
                for t in range(2):
                    pair_of_blocks(x_bank(c, X_O2 + t), t, o2T, w_o2)
                ffn(f_tile, 7)
                ffn(f_tile, 8)
                if not last:
                    pe.wait_ge(o_normed, c + 2)
                    pair_of_blocks(x_bank(c, X_OUT[0]), 0, onT, w_out)
                pe.wait_ge(xn_ready, NCH + 2 * c + 2)
                transposes(c, X_T3, xn_2)
                if not last:
                    pair_of_blocks(x_bank(c, X_OUT[1]), 1, onT, w_out)

            pe.wait_ge(o_normed, 1)
            for t in range(2):
                pair_of_blocks(X_OUT[t] % 4, t, onT, w_out)
            phase_c(0, True, False)
            phase_c(1, False, False)
            with pe.Fori(2, NCH - 1) as c:
                phase_c(c, False, False)
            phase_c(NCH - 1, False, True)
            for blk in range(BLK):
                fc(NCH - 1, blk)
            for t in range(HT + 1):
                f_tile(NCH - 1, t)


def kernel(x, ctx_1024, L0_attn_W_qkv, L0_attn_b_qkv, L0_attn_W_out, L0_attn_b_out,
           L0_xattn_Wq, L0_xattn_bq, L0_xattn_Wk, L0_xattn_bk, L0_xattn_Wv, L0_xattn_bv, L0_xattn_Wo, L0_xattn_bo,
           L0_ffn_W_fc, L0_ffn_ln_w, L0_ffn_ln_b, L0_ffn_W_proj):
    import numpy as np
    import concourse.bacc as bacc
    from concourse.bass_utils import run_bass_kernel_spmd

    def columns(v):
        return np.asarray(v).reshape(-1, P).T

    rows = np.arange(P)[:, None]
    arrays = {
        "x": np.asarray(x).reshape(T, E),
        "ctxT": np.asarray(ctx_1024).reshape(B * CTX, E).T,
        "wqkv": L0_attn_W_qkv, "bqk": columns(np.asarray(L0_attn_b_qkv)[:2 * E]), "bv": np.asarray(L0_attn_b_qkv)[2 * E:],
        "wout": L0_attn_W_out, "bout": L0_attn_b_out,
        "wqT": np.asarray(L0_xattn_Wq).T, "bq2": columns(L0_xattn_bq),
        "wkT": np.asarray(L0_xattn_Wk).T, "bk2": columns(L0_xattn_bk),
        "wvT": np.asarray(L0_xattn_Wv).T, "bv2": L0_xattn_bv,
        "woT": np.asarray(L0_xattn_Wo).T, "bo2": L0_xattn_bo,
        "wfcT": np.asarray(L0_ffn_W_fc).T, "lnw": columns(L0_ffn_ln_w), "lnb": columns(L0_ffn_ln_b),
        "wpT": np.asarray(L0_ffn_W_proj).T,
        "ident": np.eye(P, dtype=np.float32),
        "head_mask": (rows // D == np.arange(8)[None]).astype(np.float32),
        "half_mask": (rows // CTX == np.arange(2)[None]).astype(np.float32),
        "ones_bd": (rows // CTX == (np.arange(32) // D)[None]).astype(np.float32),
    }
    arrays = {f"in_{n}": np.ascontiguousarray(a) for n, a in arrays.items()}
    nc = bacc.Bacc("TRN2", target_bir_lowering=False, num_devices=1)
    args = [nc.dram_tensor(n, a.shape, mybir.dt.from_np(a.dtype), kind="ExternalInput").ap() for n, a in arrays.items()]
    out = nc.dram_tensor("out", (T, E), F32, kind="ExternalOutput").ap()
    build(nc, *args, out)
    r = run_bass_kernel_spmd(nc, [arrays], core_ids=[0])
    return r.results[0]["out"].reshape(B, S, E)
```

```python
from contextlib import ExitStack

import concourse.bass as bass
from concourse import mybir

F32 = mybir.dt.float32
BF16 = mybir.dt.bfloat16
F32R = mybir.dt.float32r
ALU = mybir.AluOpType
ACT = mybir.ActivationFunctionType
AX = mybir.AxisListType

P = 128
B, S, E = 4, 1024, 256
H, D = 16, 16
CTX = 64
F = 1024
T = B * S
CH = 512
NCH = T // CH
BLK = CH // P
KT = E // P
HG = 4
NG = H // HG
GROUPS = B * NG
KB = S // P
QC = S // CH
MSLOTS = 66
UNITS = QC * KB
MAXT = UNITS * 4
SLOTS_Q = (0, 0, 1, 1, 0, 2)
SLOTS_K = (0, 1, 0, 1, 2, 0)
STACK = len(SLOTS_Q) * D
ROWS = STACK + 3
GROUP_LOADS = 16 * (2 * len(SLOTS_Q) + 1)
HT = F // P
PAIRS = H // 2
LN_EPS = 1e-5
ABS_EPS = 1e-6

X_T2, X_Q2, X_S, X_PT, X_PV, X_O2, X_OUT, X_T3 = 0, 2, (4, 12), (8, 16), 20, 22, (24, 25), 26
X_TILES = 28
X_BEFORE = [sum(i % 4 == r for i in X_OUT) for r in range(4)]
C_LOADS = 16 * (2 * KT + 7 + 9)
O_WRITES = 16 * (HG + 1)
EARLY = 4
PREP_STEPS = 2 + 2 * B + 2 + 4 + 2
TAIL = ((2,), (3,), (4, 5), (6, 7))
SQ = QC * CH * H // P


def max_slot(t):
    return t + (t >= 8) + (t >= 40)


M_SLOTS = (41, 8)


def is_score(i):
    return any(s <= i < s + BLK for s in X_S)


def frees_before(i):
    return sum(1 for j in range(i % 4, i, 4) if not is_score(j))


X_USES = [frees_before(X_TILES + (r - X_TILES) % 4) for r in range(4)]


def free_count(c, i):
    return c * X_USES[i % 4] + frees_before(i) + X_BEFORE[i % 4]


def done_count(c, i):
    missing = sum(j <= i for j in X_OUT) if isinstance(c, int) and c == NCH - 1 else 0
    return X_TILES * c + i + 1 + len(X_OUT) - missing


def x1_count(c, k):
    r = X_OUT[k] % 4
    return c * X_USES[r] + X_BEFORE[r]


def build(nc, x, ctxT, wqkv, bqk, bv, wout, bout, wqT, bq2, wkT, bk2, wvT, bv2, woT, bo2,
          wfcT, lnw, lnb, wpT, ident_in, head_mask_in, half_mask_in, out):
    qk_scratch = nc.dram_tensor("qk_scratch", (3, 2 * E, T), BF16, kind="Internal").ap()
    v_scratch = nc.dram_tensor("v_scratch", (B, NG, P, KB, P), F32, kind="Internal").ap()
    m_scratch = nc.dram_tensor("m_scratch", (2 * GROUPS, 3, HG, CH), BF16, kind="Internal").ap()
    o_scratch = nc.dram_tensor("o_scratch", (NCH, E, CH), F32, kind="Internal").ap()
    s_scratch = nc.dram_tensor("s_scratch", (B, H, QC, CH), F32, kind="Internal").ap()
    r_scratch = nc.dram_tensor("r_scratch", (B, H, QC, CH), F32, kind="Internal").ap()

    x_v = x.rearrange("(c b p) e -> c p b e", b=BLK, p=P)
    out_v = out.rearrange("(c b p) e -> c p b e", b=BLK, p=P)

    ctx = ExitStack()
    with ctx:
        def sb(name, shape, dt=F32, where=ctx):
            return where.enter_context(nc.sbuf_tensor(name, shape, dt))

        def sem(name):
            return ctx.enter_context(nc.semaphore(name))

        ps = ctx.enter_context(nc.psum_tensor("ps", [P, 8, 512], F32))

        ident = sb("ident", [P, P])
        ident_b = sb("ident_b", [P, P], BF16)
        head_mask = sb("head_mask", [P, 8])
        half_mask = sb("half_mask", [P, 2])
        ones = sb("ones", [P, P])
        mhalf = sb("mhalf", [P, 4])
        b_qk = sb("b_qk", [P, 4])
        b_v = sb("b_v", [P, E])
        b_out = sb("b_out", [P, E])
        b_q2 = sb("b_q2", [P, 2])
        b_k2 = sb("b_k2", [P, 2])
        b_v2 = sb("b_v2", [P, E])
        b_o2 = sb("b_o2", [P, E])
        ln_w = sb("ln_w", [P, HT])
        ln_b = sb("ln_b", [P, HT])
        w_out = sb("w_out", [P, KT, E])
        w_q2 = sb("w_q2", [P, KT, E])
        w_o2 = sb("w_o2", [P, KT, E])
        t_fc = sb("t_fc", [P, KT, F])
        t_p = sb("t_p", [P, HT, E])
        b_f = sb("b_f", [P, E])
        s_c = sb("s_c", [P, B, SQ])
        abs_sum = sb("abs_sum", [P, 2])
        thr = sb("thr", [P, 3, 2])
        kbd = sb("kbd", [P, B, KT * 8 * CTX])
        vbd = sb("vbd", [P, B, PAIRS, 2 * D])
        touch = sb("touch", [P, 1])
        eps = sb("eps", [P, 4])
        stats = sb("stats", [P, 2, BLK, 6])
        mv = sb("mv", [P, 2, BLK, 2])
        veps = sb("veps", [P, 2, BLK])
        rstd = sb("rstd", [P, 2, BLK])

        ab = ctx.enter_context(ExitStack())
        xa = sb("xa", [P, BLK, E], F32, ab)
        xn_a = sb("xn_a", [P, BLK, E], F32, ab)
        xnT_a = sb("xnT_a", [P, 2, KT, CH], F32, ab)
        w_fc = sb("w_fc", [P, KT, F], F32, ab)
        w_p = sb("w_p", [P, HT, E], F32, ab)
        w_qkv = sb("w_qkv", [P, KT, 3 * E], F32, ab)
        w_k2 = sb("w_k2", [P, KT, E], F32, ab)
        w_v2 = sb("w_v2", [P, KT, E], F32, ab)
        ctx_dup = sb("ctx_dup", [P, KT, B, 2, CTX], F32, ab)
        v2b = sb("v2b", [P, E], F32, ab)
        vx = sb("vx", [P, BLK, H, 32], F32, ab)
        Qs = [sb(f"Qs{i}", [P, HG, S], BF16, ab) for i in range(NG)]
        Ks = [sb(f"Ks{i}", [P, HG, S], BF16, ab) for i in range(NG)]
        Vs = [sb(f"Vs{i}", [P, KB, P], F32, ab) for i in range(NG)]
        a_only = ab.enter_context(ExitStack())
        parts = sb("parts", [P, 4, 3, CH], BF16, a_only)
        rest = sb("rest", [P, 2, CH], F32, a_only)
        a_only.close()
        prob = sb("prob", [P, 2, 2, 2, CH], F32, ab)
        ot = sb("ot", [P, CH], F32, ab)
        maxes = sb("maxes", [P, 2, 16, 2], F32, ab)
        mrow = sb("mrow", [P, 16], F32, ab)
        mrest = sb("mrest", [P, 16], F32, ab)
        msp = sb("msp", [P, 6, 16], BF16, ab)
        mt = sb("mt", [48, P], BF16, ab)
        ab.close()

        on_raw = sb("on_raw", [P, KT, CH])
        r_raw = sb("r_raw", [P, KT, CH])
        onT = sb("onT", [P, KT, CH])
        x_in = sb("x_in", [P, BLK, E])
        x_b = sb("x_b", [P, BLK, E])
        x1 = sb("x1", [P, BLK, E])
        x1_b = sb("x1_b", [P, BLK, E])
        x2 = sb("x2", [P, BLK, E])
        x2_f = sb("x2_f", [P, 2, BLK, E])
        xn_1 = sb("xn_1", [P, BLK, E])
        xn_2 = sb("xn_2", [P, BLK, E])
        xn2T = sb("xn2T", [P, KT, CH])
        xn3T = sb("xn3T", [P, 2, KT, CH])
        q2T = sb("q2T", [P, KT, CH])
        kcur = sb("kcur", [P, KT * 8 * CTX])
        vcur = sb("vcur", [P, PAIRS, 2 * D])
        nmx = sb("nmx", [P, 2, 8])
        pe_ = sb("pe_", [P, BLK, CH])
        pT = sb("pT", [P, 2, 4, CH])
        psum = sb("psum", [P, 2, 8])
        rsum = sb("rsum", [P, 2, 8])
        o2T = sb("o2T", [P, KT, CH])
        gl = sb("gl", [P, 2, F])
        fstats = sb("fstats", [P, 2, 2, 6])
        fmv = sb("fmv", [P, 2, 2])
        fveps = sb("fveps", [P, 2])
        frstd = sb("frstd", [P, 2])
        xhat = sb("xhat", [P, BLK, F])
        xhat_last = pT[:].rearrange("p m r q -> p (m r q)").rearrange("p (b f) -> p b f", b=BLK)
        fT = sb("fT", [P, 2, 2, CH])
        xo = sb("xo", [P, BLK, E])

        a_weights = sem("a_weights")
        c_weights = sem("c_weights")
        const_set = sem("const_set")
        ident_b_set = sem("ident_b_set")
        ones_set = sem("ones_set")
        abs_summed = sem("abs_summed")
        x_loaded = sem("x_loaded")
        stats_done = sem("stats_done")
        mv_ready = sem("mv_ready")
        veps_done = sem("veps_done")
        rstd_ready = sem("rstd_ready")
        xn_ready = sem("xn_ready")
        tr_done = sem("tr_done")
        xT_copied = sem("xT_copied")
        v_mm_done = sem("v_mm_done")
        v_copied = sem("v_copied")
        v_written = sem("v_written")
        qk_mm_done = sem("qk_mm_done")
        part1_done = sem("part1_done")
        rest_done = sem("rest_done")
        part2_done = sem("part2_done")
        parts_ready = sem("parts_ready")
        parts_written = sem("parts_written")
        prep_mm = sem("prep_mm")
        prep_done = sem("prep_done")
        group_loaded = [sem(f"group_loaded{i}") for i in range(NG)]
        max_mm_done = sem("max_mm_done")
        max_reduced = sem("max_reduced")
        m_step = sem("m_step")
        m_split = sem("m_split")
        m_transposed = sem("m_transposed")
        m_copied = sem("m_copied")
        m_written = sem("m_written")
        m_loaded = sem("m_loaded")
        st_done = sem("st_done")
        exp_done = sem("exp_done")
        pv_done = sem("pv_done")
        o_copied = sem("o_copied")
        o_written = sem("o_written")
        on_loaded = sem("on_loaded")
        xc_loaded = sem("xc_loaded")
        s_loaded = sem("s_loaded")
        recip_done = sem("recip_done")
        r_written = sem("r_written")
        o_normed = sem("o_normed")
        xb_ready = sem("xb_ready")
        x1b_ready = sem("x1b_ready")
        kv_copied = sem("kv_copied")
        x2_kept = sem("x2_kept")
        x_done = sem("x_done")
        x_free = [sem(f"x_free{r}") for r in range(4)]
        exp2_done = sem("exp2_done")
        psum_done = sem("psum_done")
        rsum_done = sem("rsum_done")
        nmx_done = sem("nmx_done")
        p_ready = sem("p_ready")
        fc_done = sem("fc_done")
        gelu_done = sem("gelu_done")
        fstats_done = sem("fstats_done")
        fmv_ready = sem("fmv_ready")
        fveps_done = sem("fveps_done")
        frstd_ready = sem("frstd_ready")
        xhat_done = sem("xhat_done")
        hT_done = sem("hT_done")
        xh_high = sem("xh_high")
        fh_ready = sem("fh_ready")
        ft_ready = sem("ft_ready")
        acc_done = sem("acc_done")
        out_added = sem("out_added")
        out_written = sem("out_written")

        block = ctx.enter_context(nc.Block())

        @block.sync
        def _(sp):
            for n, (t, d) in enumerate(((ident, ident_in), (w_qkv, wqkv.rearrange("(k p) n -> p k n", p=P)),
                                        (b_qk, bqk), (b_v, bv.partition_broadcast(P)))):
                sp.dma_start(t[:], d).then_inc(a_weights, 16)

            def phase_a(c, last):
                b, kb = c // 2, (c % 2) * BLK
                sp.wait_ge(v_copied, 2 * c + 2)
                for g in range(NG):
                    sp.dma_start(v_scratch[b, g, :, bass.ds(kb, BLK), :],
                                 vx[:, :, g * HG:(g + 1) * HG, :].rearrange("p b h d -> p b (h d)")
                                 ).then_inc(v_written, 16)
                for m in range(4):
                    sp.wait_ge(parts_ready, 4 * c + m + 1)
                    sp.dma_start(qk_scratch[:, m * P:(m + 1) * P, bass.ts(c, CH)].rearrange("s p t -> p s t"),
                                 parts[:, m]).then_inc(parts_written, 16)

            def load_group(b, g):
                for slots, base, dst in ((SLOTS_Q, 0, Qs[g]), (SLOTS_K, E, Ks[g])):
                    for i, part in enumerate(slots):
                        rows = qk_scratch[part, base + g * HG * D:base + (g + 1) * HG * D, bass.ts(b, S)]
                        sp.dma_start(dst[i * D:(i + 1) * D, :, :],
                                     rows.rearrange("(j d) t -> d j t", d=D)).then_inc(group_loaded[g], 16)
                sp.dma_start(Vs[g][:], v_scratch[b, g]).then_inc(group_loaded[g], 16)

            phase_a(0, False)
            with sp.Fori(1, 3) as c:
                phase_a(c, False)
            for g in range(3):
                c = 3 + g
                sp.wait_ge(v_written, 16 * NG * c)
                sp.wait_ge(parts_written, 16 * 4 * c)
                load_group(0, g)
                phase_a(c, False)
            with sp.Fori(6, NCH) as c:
                phase_a(c, False)
            sp.wait_ge(v_written, 16 * NG * NCH)
            sp.wait_ge(parts_written, 16 * 4 * NCH)

            def m_rows(f, g, qc):
                sp.wait_ge(m_copied, f + 1)
                sp.dma_start(m_scratch[f].rearrange("s j (k q) -> (s j k) q", q=P), mt[:]).then_inc(m_written, 16)
                sp.wait_ge(m_written, 16 * (f + 1))
                sp.dma_start(Qs[g][STACK:ROWS, :, qc * CH:(qc + 1) * CH], m_scratch[f]).then_inc(m_loaded, 16)

            def sums(scratch, b):
                return scratch[b].rearrange("h c (s q) -> (h c s) q", q=SQ)

            def r_write(b):
                sp.dma_start(sums(r_scratch, b), s_c[:, b, :]).then_inc(r_written, 16)

            def load_o(b, qc):
                sp.dma_start(on_raw[:], o_scratch[b * QC + qc].rearrange("(k p) t -> p k t", p=P)).then_inc(on_loaded, 16)
                for k in range(KT):
                    sp.dma_start(r_raw[:, k, :], r_scratch[b, k * 8:(k + 1) * 8, qc, None, :].broadcast_to([8, D, CH])
                                 ).then_inc(on_loaded, 16)

            def load_xc(c):
                sp.dma_start(x_in[:], x_v[c]).then_inc(xc_loaded, 16)

            def o_write(G, b, g, qc):
                sp.wait_ge(o_copied, 2 * G + qc + 1)
                for j in range(HG):
                    rows = slice((g * HG + j) * D, (g * HG + j + 1) * D)
                    sp.dma_start(o_scratch[b * QC + qc, rows, :], ot[32 * j:32 * j + D, :]).then_inc(o_written, 16)
                sp.dma_start(s_scratch[b, g * HG:(g + 1) * HG, qc, :], ot[D:P:2 * D, :]).then_inc(o_written, 16)

            m_rows(0, 0, 0)

            def phase_b(b, last):
                for g in range(NG):
                    G = b * NG + g
                    if not last or g == 0:
                        sp.wait_ge(pv_done, UNITS * G)
                        load_group(b + (g + 3) // NG, (g + 3) % NG)
                    if last and g == 0:
                        sp.wait_ge(o_written, O_WRITES * 2 * NG * (B - 1))
                        for i in range(B - 1):
                            sp.dma_start(s_c[:, i, :], sums(s_scratch, i)).then_inc(s_loaded, 16)
                    m_rows(2 * G + 1, g, 1)
                    if last and g == NG - 1:
                        sp.wait_ge(recip_done, 1)
                        for i in range(B - 1):
                            r_write(i)
                        sp.wait_ge(r_written, 16 * (B - 1))
                        load_o(0, 0)
                        load_xc(0)
                    o_write(G, b, g, 0)
                    if not (last and g == NG - 1):
                        m_rows(2 * G + 2, (g + 1) % NG, 0)
                    o_write(G, b, g, 1)

            phase_b(0, False)
            with sp.Fori(1, B - 1) as b:
                phase_b(b, False)
            phase_b(B - 1, True)

            sp.wait_ge(o_written, O_WRITES * 2 * GROUPS)
            sp.dma_start(s_c[:, B - 1, :], sums(s_scratch, B - 1)).then_inc(s_loaded, 16)

            def write_out(c):
                sp.wait_ge(out_added, 2 * c + 2)
                sp.dma_start(out_v[c], xo[:]).then_inc(out_written, 16)

            def phase_c(c, b, qc, first=False, last=False):
                if not last:
                    sp.wait_ge(o_normed, c + 1)
                    load_o(b, qc)
                    sp.wait_ge(xb_ready, c + 1)
                    load_xc(c + 1)
                if not first:
                    write_out(c - 2)

            phase_c(0, 0, 1, first=True)
            sp.wait_ge(recip_done, 2)
            r_write(B - 1)
            sp.wait_ge(r_written, 16 * B)
            phase_c(1, 1, 0, first=True)
            with sp.Fori(1, B - 1) as b:
                phase_c(2 * b, b, 1)
                phase_c(2 * b + 1, b + 1, 0)
            phase_c(NCH - 2, B - 1, 1)
            phase_c(NCH - 1, None, None, last=True)
            write_out(NCH - 2)
            write_out(NCH - 1)
            sp.wait_ge(out_written, 16 * NCH)

        @block.gpsimd
        def _(pool):
            pool.dma_start(xa[:], x_v[0]).then_inc(x_loaded, 16)
            pool.memset(ones[:], 1.0).then_inc(const_set, 1)
            pool.memset(mhalf[:], -0.5).then_inc(const_set, 1)
            pool.memset(eps[:], LN_EPS).then_inc(const_set, 1)
            pool.memset(msp[:], 0.0).then_inc(const_set, 1)
            pool.wait_ge(const_set, 4)
            def make_rstd(n, par=0):
                pool.wait_ge(mv_ready, n + 1)
                pool.tensor_tensor(veps[:, par], mv[:, par, :, 1], eps[:], ALU.add).then_inc(veps_done, 1)
                pool.wait_ge(veps_done, n + 1)
                pool.tensor_tensor(rstd[:, par], veps[:, par], mhalf[:], ALU.pow).then_inc(rstd_ready, 1)

            def part3(c, m):
                pool.wait_ge(part2_done, 4 * c + m + 1)
                pool.tensor_tensor(parts[:, m, 2, :], rest[:, m % 2, :], parts[:, m, 1, :],
                                   ALU.subtract).then_inc(parts_ready, 1)

            def phase_a(c, last=False):
                if not last:
                    make_rstd(c + 1)
                part3(c, 0)
                if not last:
                    pool.wait_ge(xn_ready, c + 2)
                    if not (isinstance(c, int) and c == NCH - 2):
                        pool.dma_start(xa[:], x_v[c + 2]).then_inc(x_loaded, 16)
                for m in range(1, 4):
                    part3(c, m)

            make_rstd(0)
            pool.wait_ge(xn_ready, 1)
            pool.dma_start(xa[:], x_v[1]).then_inc(x_loaded, 16)
            for g in range(NG):
                pool.wait_ge(const_set, 4 + g)
                pool.memset(Ks[g][STACK:ROWS, :, :], 1.0).then_inc(const_set, 1)
            pool.wait_ge(const_set, 4 + NG)
            phase_a(0)
            with pool.Fori(1, NCH - 2) as c:
                phase_a(c)
            phase_a(NCH - 2)
            phase_a(NCH - 1, True)

            def f_rstd(c, blk):
                n = BLK * c + blk
                s = blk % 2
                pool.wait_ge(fmv_ready, n + 1)
                pool.tensor_tensor(fveps[:, s:s + 1], fmv[:, s, 1:2], eps[:, 0:1], ALU.add).then_inc(fveps_done, 1)
                pool.wait_ge(fveps_done, n + 1)
                pool.tensor_tensor(frstd[:, s:s + 1], fveps[:, s:s + 1], mhalf[:, 0:1], ALU.pow).then_inc(frstd_ready, 1)

            def x_plus_b(c):
                pool.wait_ge(xc_loaded, 16 * (c + 1))
                pool.tensor_tensor(x_b[:], x_in[:], b_out[:, None, :].broadcast_to([P, BLK, E]),
                                   ALU.add).then_inc(xb_ready, 1)

            def normalise(c):
                pool.wait_ge(on_loaded, 16 * (1 + KT) * (c + 1))
                pool.tensor_tensor(onT[:], on_raw[:], r_raw[:], ALU.mult).then_inc(o_normed, 1)

            def probabilities(c, m, blk):
                n = 8 * c + 4 * m + blk
                pool.wait_ge(rsum_done, n + 1)
                p = pe_[:, blk, :].rearrange("p (h t) -> p h t", h=8)
                pool.tensor_tensor(p, p, rsum[:, blk % 2, :, None].broadcast_to([P, 8, CTX]), ALU.mult).then_inc(p_ready, 1)

            def x1_plus_b(c):
                for k in range(2):
                    pool.wait_ge(x_free[X_OUT[k] % 4], x1_count(c, k))
                pool.tensor_tensor(x1_b[:], x1[:], b_o2[:, None, :].broadcast_to([P, BLK, E]),
                                   ALU.add).then_inc(x1b_ready, 1)

            def x2_plus_b(c, c_min):
                if c_min >= 2:
                    pool.wait_ge(out_added, 2 * (c - 1))
                for i in (X_O2, X_O2 + 1):
                    pool.wait_ge(x_free[i % 4], free_count(c, i) + 1)
                pool.tensor_tensor(x2_f[:, c_min % 2], x2[:], b_f[:, None, :].broadcast_to([P, BLK, E]),
                                   ALU.add).then_inc(x2_kept, 1)

            normalise(0)
            pool.wait_ge(c_weights, C_LOADS)
            pool.wait_ge(prep_done, PREP_STEPS)
            x_plus_b(0)
            make_rstd(NCH)

            def phase_c(c, c_min=2, last=False):
                def ffn(blk):
                    if c_min >= 1:
                        f_rstd(c - 1, blk)
                x1_plus_b(c)
                if not last:
                    x_plus_b(c + 1)
                    normalise(c + 1)
                for m in range(KT):
                    for blk in range(BLK):
                        probabilities(c, m, blk)
                for blk in range(BLK):
                    ffn(blk)
                make_rstd(NCH + 2 * c + 1, 1)
                if not last:
                    make_rstd(NCH + 2 * c + 2)
                x2_plus_b(c, c_min)

            phase_c(0, 0)
            phase_c(1, 1)
            with pool.Fori(1, B - 1) as b:
                phase_c(2 * b, 2)
                phase_c(2 * b + 1, 3)
            phase_c(NCH - 2, 2)
            phase_c(NCH - 1, 3, last=True)
            for blk in range(BLK):
                f_rstd(NCH - 1, blk)

        @block.scalar
        def _(act):
            for h in range(2):
                for k in range(KT):
                    act.dma_start(ctx_dup[:, k, :, h, :],
                                  ctxT[k * P:(k + 1) * P, :].rearrange("p (b t) -> p b t", b=B)).then_inc(c_weights, 16)
            for t, d in ((w_out, wout), (w_q2, wqT), (w_k2, wkT), (w_v2, wvT), (w_o2, woT), (w_fc, wfcT), (w_p, wpT)):
                act.dma_start(t[:], d.rearrange("(k p) n -> p k n", p=P)).then_inc(c_weights, 16)
            for t, d in ((b_q2, bq2), (b_k2, bk2), (ln_w, lnw), (ln_b, lnb), (head_mask, head_mask_in),
                         (half_mask, half_mask_in), (b_out, bout.partition_broadcast(P)),
                         (b_v2, bv2.partition_broadcast(P)), (b_o2, bo2.partition_broadcast(P))):
                act.dma_start(t[:], d).then_inc(c_weights, 16)
            act.wait_ge(a_weights, 16 * 4)
            act.activation(ident_b[:], ident[:], ACT.Copy).then_inc(ident_b_set, 1)

            def xT_copy(c, par):
                for k in range(KT):
                    act.wait_ge(tr_done, 2 * c + k + 1)
                    act.activation(xnT_a[:, par, k, :], ps[:, k, :], ACT.Copy).then_inc(xT_copied, 1)

            def part1(c, m):
                act.wait_ge(qk_mm_done, 4 * c + m + 1)
                if m == 0:
                    act.wait_ge(parts_written, 16 * 4 * c)
                act.activation(parts[:, m, 0, :], ps[:, 4 + m, :], ACT.Identity,
                               bias=b_qk[:, m:m + 1]).then_inc(part1_done, 1)

            def part2(c, m):
                act.wait_ge(rest_done, 4 * c + m + 1)
                act.activation(parts[:, m, 1, :], rest[:, m % 2, :], ACT.Copy).then_inc(part2_done, 1)

            def phase_a(c, par, last=False):
                part1(c, 0)
                if not last:
                    xT_copy(c + 1, 1 - par)
                part2(c, 0)
                part1(c, 1)
                part1(c, 2)
                part2(c, 1)
                part1(c, 3)
                part2(c, 2)
                part2(c, 3)

            xT_copy(0, 0)
            phase_a(0, 0)
            with act.Fori(1, NCH - 1, 2) as c:
                phase_a(c, 1)
                phase_a(c + 1, 0)
            phase_a(NCH - 1, 1, True)

            junk = vx[:].rearrange("p b h d -> p (b h d)")
            act.wait_ge(v_written, 16 * NG * NCH)
            act.wait_ge(c_weights, C_LOADS)
            for i, w in enumerate((w_fc, w_p)):
                act.wait_ge(abs_summed, i)
                act.activation(junk, w[:].rearrange("p k n -> p (k n)"), ACT.Abs,
                               accum_out=abs_sum[:, i:i + 1]).then_inc(abs_summed, 1)

            def m_copy(f, qc):
                act.wait_ge(m_transposed, f + 1)
                act.wait_ge(m_written, 16 * f)
                act.activation(mt[:], ps[:, 5 + M_SLOTS[qc] % 3, :].bitcast(BF16)[0:48, 0:P], ACT.Copy).then_inc(m_copied, 1)

            def exps(U, par):
                for h in range(2):
                    act.wait_ge(st_done, 2 * U + h + 1)
                    act.activation(prob[:, par, h].rearrange("p a q -> p (a q)"),
                                   ps[:, 2 * h:2 * h + 2, :].rearrange("p a q -> p (a q)"),
                                   ACT.Exp).then_inc(exp_done, 1)

            act.wait_ge(abs_summed, 2)
            m_copy(0, 0)
            exps(0, 0)

            def phase_b(b, last):
                for g in range(NG):
                    G = b * NG + g
                    end = last and g == NG - 1
                    for s in range(UNITS):
                        U = G * UNITS + s
                        if s == 2:
                            m_copy(2 * G + 1, 1)
                        if s == 10 and not end:
                            m_copy(2 * G + 2, 0)
                        if not (end and s == UNITS - 1):
                            act.wait_ge(pv_done, U)
                            exps(U + 1, (s + 1) % 2)
                        if s % KB == KB - 1:
                            qc = s // KB
                            act.wait_ge(pv_done, U + 1)
                            act.wait_ge(o_written, O_WRITES * (2 * G + qc))
                            act.activation(ot[:], ps[:, 4, :], ACT.Copy).then_inc(o_copied, 1)

            phase_b(0, False)
            with act.Fori(1, B - 1) as b:
                phase_b(b, False)
            phase_b(B - 1, True)

            def x_ready(c, i):
                act.wait_ge(x_done, done_count(c, i))

            def x_copy(c, i, dst, done=None):
                x_ready(c, i)
                act.activation(dst, ps[:, i % 4, :], ACT.Copy).then_inc(done or x_free[i % 4], 1)

            def gelu(c, blk, base=4):
                act.wait_ge(fc_done, BLK * c + blk + 1)
                act.wait_ge(xhat_done, BLK * c + max(blk - 1, 0))
                r = base + 2 * (blk % 2)
                act.activation(gl[:, blk % 2, :], ps[:, r:r + 2, :].rearrange("p a q -> p (a q)"),
                               ACT.Gelu).then_inc(gelu_done, 1)

            def ft_high(c, t):
                act.wait_ge(hT_done, HT * c + t + 1)
                act.activation(fT[:, t % 2, 0, :].bitcast(F32R), ps[:, 4 + t % 2, :], ACT.Identity,
                               scale=ln_w[:, t:t + 1]).then_inc(fh_ready, 1)

            def c_exp(c, m, blk):
                act.wait_ge(nmx_done, 8 * c + 4 * m + blk + 1)
                i = X_S[m] + blk
                for h in range(8):
                    a = act.activation(pe_[:, blk, h * CTX:(h + 1) * CTX], ps[:, i % 4, h * CTX:(h + 1) * CTX], ACT.Exp,
                                       bias=nmx[:, blk % 2, h:h + 1])
                a.then_inc(exp2_done, 1)

            def keys_and_values(b):
                act.activation(kcur[:], kbd[:, b], ACT.Copy).then_inc(kv_copied, 1)
                act.activation(vcur[:], vbd[:, b], ACT.Copy).then_inc(kv_copied, 1)

            def phase_c(c, b, c_min=2, last=False):
                def second(f, *a):
                    if c_min >= 2:
                        f(c - 2, *a)

                def first(f, *a):
                    if c_min >= 1:
                        f(c - 1, *a)

                def pT_copy(m, blk):
                    i = X_PT[m] + blk
                    x_ready(c, i)
                    act.activation(pT[:, m, :, blk * P:(blk + 1) * P],
                                   ps[:, i % 4, :].rearrange("p (r q) -> p r q", r=4),
                                   ACT.Copy).then_inc(x_free[i % 4], 1)

                second(ft_high, 2)
                for k in range(KT):
                    x_copy(c, X_T2 + k, xn2T[:, k, :])
                second(ft_high, 3)
                for m in range(KT):
                    x_ready(c, X_Q2 + m)
                    act.activation(q2T[:, m, :], ps[:, (X_Q2 + m) % 4, :], ACT.Identity,
                                   scale=float(D) ** -0.5, bias=b_q2[:, m:m + 1]).then_inc(x_free[(X_Q2 + m) % 4], 1)
                c_exp(c, 0, 0)
                second(ft_high, 4)
                c_exp(c, 0, 1)
                second(ft_high, 5)
                c_exp(c, 0, 2)
                pT_copy(0, 0)
                c_exp(c, 0, 3)
                pT_copy(0, 1)
                second(ft_high, 6)
                pT_copy(0, 2)
                pT_copy(0, 3)
                c_exp(c, 1, 0)
                second(ft_high, 7)
                c_exp(c, 1, 1)
                c_exp(c, 1, 2)
                c_exp(c, 1, 3)
                pT_copy(1, 0)
                pT_copy(1, 1)
                first(gelu, 0)
                first(gelu, 1)
                pT_copy(1, 2)
                pT_copy(1, 3)
                for k in range(KT):
                    x_copy(c, X_PV + k, o2T[:, k, :])
                first(gelu, 2)
                first(gelu, 3)
                if not last:
                    keys_and_values(b)
                first(ft_high, 0)
                first(ft_high, 1)
                for k in range(KT):
                    x_copy(c, X_T3 + k, xn3T[:, 0, k, :].bitcast(F32R), xh_high)

            act.wait_ge(prep_done, PREP_STEPS)
            keys_and_values(0)
            phase_c(0, 0, 0)
            phase_c(1, 1, 1)
            with act.Fori(1, B - 1) as b:
                phase_c(2 * b, b)
                phase_c(2 * b + 1, b + 1)
            phase_c(NCH - 2, B - 1)
            phase_c(NCH - 1, None, last=True)
            for blk in range(BLK):
                for t in TAIL[blk]:
                    ft_high(NCH - 2, t)
                gelu(NCH - 1, blk, 0)
            for t in range(HT):
                ft_high(NCH - 1, t)

        @block.vector
        def _(dve):
            dve.memset(vx[:, :, :, D:32], float(E) ** 0.5).then_inc(ones_set, 1)

            def ln_stats(n, src, par=0):
                for blk in range(BLK):
                    i = dve.bn_stats(stats[:, par, blk, :], src[:, blk, :])
                i.then_inc(stats_done, 1)
                dve.wait_ge(stats_done, n + 1)
                dve.tensor_copy(touch[:], stats[:, par, 0, 0:1])
                for blk in range(BLK):
                    i = dve.bn_aggr(mv[:, par, blk, :], stats[:, par, blk, :])
                i.then_inc(mv_ready, 1)

            def ln_apply(n, src, dst, par=0):
                dve.wait_ge(rstd_ready, n + 1)
                for blk in range(BLK):
                    i = dve.tensor_scalar(dst[:, blk, :], src[:, blk, :], mv[:, par, blk, 0:1], rstd[:, par, blk:blk + 1],
                                          ALU.subtract, ALU.mult)
                i.then_inc(xn_ready, 1)

            def a_stats(c):
                dve.wait_ge(x_loaded, 16 * (c + 1))
                ln_stats(c, xa)

            def a_apply(c):
                dve.wait_ge(tr_done, 2 * c)
                ln_apply(c, xa, xn_a)

            def v_copy(c, i):
                if i == 0:
                    dve.wait_ge(v_written, 16 * NG * c)
                dve.wait_ge(v_mm_done, 2 * c + i + 1)
                dve.tensor_tensor(vx[:, 2 * i:2 * i + 2, :, 0:D],
                                  ps[:, 2, :].rearrange("p (b h d) -> p b h d", b=2, h=H),
                                  b_v[:].rearrange("p (b h d) -> p b h d", b=1, h=H).broadcast_to([P, 2, H, D]),
                                  ALU.add).then_inc(v_copied, 1)

            def reduce_tile(G, t, early=False):
                dve.wait_ge(max_mm_done, MAXT * G + t + 1)
                qc, i = divmod(t, MAXT // 2)
                dve.tensor_reduce(maxes[:, qc, i // 2, i % 2:i % 2 + 1], ps[:, 3 if early else 5 + max_slot(t) % 3, :], AX.X,
                                  ALU.max).then_inc(max_reduced, 1)

            def rest1(c, m):
                dve.wait_ge(parts_ready, 4 * c + max(m - 1, 0))
                dve.wait_ge(part1_done, 4 * c + m + 1)
                dve.scalar_tensor_tensor(out=rest[:, m % 2, :], in0=ps[:, 4 + m, :], scalar=b_qk[:, m:m + 1],
                                         in1=parts[:, m, 0, :], op0=ALU.add, op1=ALU.subtract).then_inc(rest_done, 1)

            def phase_a(c, last=False, early=None):
                def reduce_early(k):
                    if early is not None:
                        reduce_tile(0, early + k, True)
                if not last:
                    a_stats(c + 1)
                reduce_early(0)
                v_copy(c, 0)
                reduce_early(1)
                if not last:
                    a_apply(c + 1)
                v_copy(c, 1)
                reduce_early(2)
                reduce_early(3)
                for m in range(4):
                    rest1(c, m)
                    reduce_early(4 + m)

            a_stats(0)
            a_apply(0)
            dve.wait_ge(a_weights, 16 * 4)
            dve.wait_ge(ones_set, 1)
            phase_a(0)
            with dve.Fori(1, EARLY) as c:
                phase_a(c)
            for c in range(EARLY, NCH):
                phase_a(c, c == NCH - 1, 8 * (c - EARLY))

            def split_max(f, qc, step):
                if step == 0:
                    dve.wait_ge(max_reduced, (MAXT // 2) * (f + 1))
                    dve.tensor_tensor(mrow[:], maxes[:, qc, :, 0], maxes[:, qc, :, 1], ALU.max).then_inc(m_step, 1)
                elif step == 1:
                    dve.wait_ge(m_step, 3 * f + 1)
                    dve.wait_ge(m_transposed, f)
                    dve.tensor_scalar(msp[:, 0, :], mrow[:], -1.0, None, ALU.mult).then_inc(m_step, 1)
                elif step == 2:
                    dve.wait_ge(m_step, 3 * f + 2)
                    dve.scalar_tensor_tensor(out=mrest[:], in0=mrow[:], scalar=-1.0, in1=msp[:, 0, :],
                                             op0=ALU.mult, op1=ALU.subtract).then_inc(m_step, 1)
                elif step == 3:
                    dve.wait_ge(m_step, 3 * f + 3)
                    dve.tensor_copy(msp[:, 1, :], mrest[:]).then_inc(m_split, 1)
                else:
                    dve.wait_ge(m_split, 2 * f + 1)
                    dve.tensor_tensor(msp[:, 2, :], mrest[:], msp[:, 1, :], ALU.subtract).then_inc(m_split, 1)

            def max_pass(G, start=0):
                for t in range(start, MAXT):
                    reduce_tile(G, t)
                    if t % (MAXT // 2) < 5:
                        if t >= MAXT // 2:
                            split_max(2 * G, 0, t - MAXT // 2)
                        else:
                            split_max(2 * G - 1, 1, t)

            max_pass(0, MAXT // 2)

            def phase_b(b, last):
                for g in range(NG - 1 if last else NG):
                    max_pass(b * NG + g + 1)

            phase_b(0, False)
            with dve.Fori(1, B - 1) as b:
                phase_b(b, False)
            phase_b(B - 1, True)
            for step in range(5):
                split_max(2 * GROUPS - 1, 1, step)

            def reciprocals(n, lo, hi):
                dve.wait_ge(s_loaded, 16 * hi)
                dve.reciprocal(s_c[:, lo:hi, :], s_c[:, lo:hi, :]).then_inc(recip_done, 1)

            reciprocals(0, 0, B - 1)

            dve.wait_ge(c_weights, C_LOADS)
            n = 0
            dve.wait_ge(prep_mm, 1)
            for m in range(KT):
                src = ps[:, 5, m * B * CTX:(m + 1) * B * CTX].rearrange("p (b t) -> p b t", b=B)
                for h in range(8):
                    i = dve.tensor_scalar(kbd[:, :, (m * 8 + h) * CTX:(m * 8 + h + 1) * CTX], src, b_k2[:, m:m + 1], head_mask[:, h:h + 1],
                                          ALU.add, ALU.mult)
            i.then_inc(prep_done, 1)
            n += 1
            dve.tensor_scalar(b_q2[:], b_q2[:], float(D) ** -0.5, None, ALU.mult).then_inc(prep_done, 1)
            n += 1
            for b in range(B):
                dve.wait_ge(prep_mm, 2 + b // 2)
                dve.tensor_tensor(v2b[:], ps[:, 6 + b // 2, (b % 2) * E:(b % 2 + 1) * E], b_v2[:],
                                  ALU.add).then_inc(prep_done, 1)
                n += 1
                dve.wait_ge(prep_done, n)
                v2v = v2b[:].rearrange("p (r h d) -> p r h d", r=PAIRS, h=2)
                for h in range(2):
                    i = dve.tensor_scalar(vbd[:, b, :, h * D:(h + 1) * D], v2v[:, :, h, :], half_mask[:, h:h + 1], None, ALU.mult)
                i.then_inc(prep_done, 1)
                n += 1
                dve.wait_ge(prep_done, n)
            dve.wait_ge(prep_mm, 4)
            dve.tensor_scalar(thr[:, 0, :], ps[:, 5, 0:2], 1.0 / (E * F), ABS_EPS, ALU.mult, ALU.add).then_inc(prep_done, 1)
            n += 1
            dve.wait_ge(prep_done, n)
            dve.tensor_scalar(thr[:, 1, :], thr[:, 0, :], 0.5, None, ALU.mult)
            dve.tensor_scalar(thr[:, 2, :], thr[:, 0, :], -0.5, None, ALU.mult).then_inc(prep_done, 1)
            n += 1
            dve.wait_ge(prep_done, n)
            neg = vx[:].rearrange("p b h d -> p (b h d)")
            for i, (w, ternary) in enumerate(((w_fc, t_fc), (w_p, t_p))):
                wf = w[:].rearrange("p k n -> p (k n)")
                dve.tensor_scalar(neg, wf, thr[:, 2, i:i + 1], None, ALU.is_lt).then_inc(prep_done, 1)
                n += 1
                dve.wait_ge(prep_done, n)
                dve.scalar_tensor_tensor(out=ternary[:].rearrange("p k n -> p (k n)").bitcast(F32R), in0=wf,
                                         scalar=thr[:, 1, i:i + 1], in1=neg,
                                         op0=ALU.is_gt, op1=ALU.subtract).then_inc(prep_done, 1)
                n += 1
                dve.wait_ge(prep_done, n)
            dve.tensor_tensor(vx[:, 0:2].rearrange("p b h d -> p (b h d)").rearrange("p (t c) -> p t c", t=HT),
                              ln_b[:, :, None].broadcast_to([P, HT, P]),
                              ones[:, None, :].broadcast_to([P, HT, P]), ALU.mult).then_inc(prep_done, 1)
            n += 1
            dve.wait_ge(prep_mm, 5)
            dve.tensor_copy(b_f[:], ps[:, 6, 0:E]).then_inc(prep_done, 1)
            n += 1
            assert n == PREP_STEPS

            def x_ready(c, i):
                dve.wait_ge(x_done, done_count(c, i))

            def add_tile(c, i, dst, src, k):
                x_ready(c, i)
                dve.tensor_tensor(dst[:, 2 * k:2 * k + 2, :], ps[:, i % 4, :].rearrange("p (b e) -> p b e", b=2),
                                  src[:, 2 * k:2 * k + 2, :], ALU.add).then_inc(x_free[i % 4], 1)

            def x_sums(c, m, blk):
                n = 8 * c + 4 * m + blk
                dve.wait_ge(exp2_done, n + 1)
                dve.tensor_reduce(psum[:, blk % 2, :], pe_[:, blk, :].rearrange("p (h t) -> p h t", h=8), AX.X,
                                  ALU.add).then_inc(psum_done, 1)

            def x_recip(c, m, blk, first):
                n = 8 * c + 4 * m + blk
                if not first or 4 * m + blk >= 2:
                    dve.wait_ge(p_ready, n - 1)
                dve.wait_ge(psum_done, n + 1)
                dve.reciprocal(rsum[:, blk % 2, :], psum[:, blk % 2, :]).then_inc(rsum_done, 1)

            def scores(c, m, blk, first):
                i = X_S[m] + blk
                s = ps[:, i % 4, :].rearrange("p (h t) -> p h t", h=8)
                x_ready(c, i)
                k = blk % 2
                if not first or 4 * m + blk >= 2:
                    dve.wait_ge(exp2_done, 8 * c + 4 * m + blk - 1)
                dve.tensor_reduce(nmx[:, k, :], s, AX.X, ALU.max, negate=True).then_inc(nmx_done, 1)
                if blk:
                    x_sums(c, m, blk - 1)
                    x_recip(c, m, blk - 1, first)

            def f_stats(c, blk):
                n = BLK * c + blk
                k = blk % 2
                dve.wait_ge(gelu_done, n + 1)
                for h in range(2):
                    i = dve.bn_stats(fstats[:, k, h, :], gl[:, k, h * 512:(h + 1) * 512])
                i.then_inc(fstats_done, 1)
                dve.wait_ge(fstats_done, n + 1)
                dve.tensor_copy(touch[:], fstats[:, k, 0, 0:1])
                dve.bn_aggr(fmv[:, k, :], fstats[:, k, :, :]).then_inc(fmv_ready, 1)

            def f_apply(c, blk, dst=xhat):
                k = blk % 2
                dve.wait_ge(frstd_ready, BLK * c + blk + 1)
                dve.tensor_scalar(dst[:, blk, :], gl[:, k, :], fmv[:, k, 0:1], frstd[:, k:k + 1],
                                  ALU.subtract, ALU.mult).then_inc(xhat_done, 1)

            def x1_half(c, k):
                r = X_OUT[k] % 4
                dve.wait_ge(x_done, (k + 1) if isinstance(c, int) and c == 0 else done_count(c - 1, X_OUT[k]))
                dve.tensor_tensor(x1[:, 2 * k:2 * k + 2, :], ps[:, r, :].rearrange("p (b e) -> p b e", b=2),
                                  x_b[:, 2 * k:2 * k + 2, :], ALU.add).then_inc(x_free[r], 1)

            def x1_stats(c):
                for k in range(2):
                    dve.wait_ge(x_free[X_OUT[k] % 4], x1_count(c, k))
                ln_stats(NCH + 2 * c, x1)

            def ft_low(c, t):
                dve.wait_ge(fh_ready, HT * c + t + 1)
                dve.scalar_tensor_tensor(out=fT[:, t % 2, 1, :].bitcast(F32R), in0=ps[:, 4 + t % 2, :],
                                         scalar=ln_w[:, t:t + 1], in1=fT[:, t % 2, 0, :],
                                         op0=ALU.mult, op1=ALU.subtract).then_inc(ft_ready, 1)

            def x3_low(c):
                for k in range(KT):
                    i = X_T3 + k
                    dve.wait_ge(xh_high, KT * c + k + 1)
                    dve.tensor_tensor(xn3T[:, 1, k, :].bitcast(F32R), ps[:, i % 4, :], xn3T[:, 0, k, :],
                                      ALU.subtract).then_inc(x_free[i % 4], 1)

            def f_out(c, par):
                dve.wait_ge(acc_done, c + 1)
                dve.wait_ge(x2_kept, c + 1)
                dve.wait_ge(out_written, 16 * c)
                for i in range(2):
                    dve.tensor_tensor(xo[:, 2 * i:2 * i + 2, :], ps[:, 6 + i, :].rearrange("p (b e) -> p b e", b=2),
                                      x2_f[:, par, 2 * i:2 * i + 2, :], ALU.add).then_inc(out_added, 1)

            dve.wait_ge(xb_ready, 1)
            for k in range(2):
                x1_half(0, k)
            x1_stats(0)

            def phase_c(c, c_min=2, last=False):
                def second(f, *a):
                    if c_min >= 2:
                        f(c - 2, *a)

                def first(f, *a):
                    if c_min >= 1:
                        f(c - 1, *a)

                fresh = c_min == 0
                ln_apply(NCH + 2 * c, x1, xn_1)
                for t in range(2, 4):
                    second(ft_low, t)
                scores(c, 0, 0, fresh)
                scores(c, 0, 1, fresh)
                second(ft_low, 4)
                scores(c, 0, 2, fresh)
                second(ft_low, 5)
                scores(c, 0, 3, fresh)
                if fresh:
                    reciprocals(1, B - 1, B)
                x_sums(c, 0, 3)
                x_recip(c, 0, 3, fresh)
                second(ft_low, 6)
                scores(c, 1, 0, fresh)
                scores(c, 1, 1, fresh)
                second(ft_low, 7)
                scores(c, 1, 2, fresh)
                second(f_out, c_min % 2)
                scores(c, 1, 3, fresh)
                x_sums(c, 1, 3)
                x_recip(c, 1, 3, fresh)
                first(f_stats, 0)
                first(f_stats, 1)
                first(f_apply, 0)
                first(f_apply, 1)
                first(f_stats, 2)
                dve.wait_ge(x1b_ready, c + 1)
                if not fresh:
                    dve.wait_ge(x2_kept, c)
                add_tile(c, X_O2, x2, x1_b, 0)
                first(f_apply, 2)
                add_tile(c, X_O2 + 1, x2, x1_b, 1)
                first(f_stats, 3)
                for i in (X_O2, X_O2 + 1):
                    dve.wait_ge(x_free[i % 4], free_count(c, i) + 1)
                ln_stats(NCH + 2 * c + 1, x2, 1)
                first(f_apply, 3)
                if not last:
                    dve.wait_ge(xb_ready, c + 2)
                    for k in range(2):
                        x1_half(c + 1, k)
                first(ft_low, 0)
                if not last:
                    x1_stats(c + 1)
                first(ft_low, 1)
                ln_apply(NCH + 2 * c + 1, x2, xn_2, 1)
                x3_low(c)

            phase_c(0, 0)
            phase_c(1, 1)
            with dve.Fori(1, B - 1) as b:
                phase_c(2 * b, 2)
                phase_c(2 * b + 1, 3)
            phase_c(NCH - 2, 2)
            phase_c(NCH - 1, 3, last=True)
            for blk in range(BLK):
                for t in TAIL[blk]:
                    if t > 1:
                        ft_low(NCH - 2, t)
                f_stats(NCH - 1, blk)
                f_apply(NCH - 1, blk, xhat_last)
            f_out(NCH - 2, 0)
            for t in range(HT):
                ft_low(NCH - 1, t)
            f_out(NCH - 1, 1)

        @block.tensor
        def _(pe):
            def mm(o, lhsT, rhs, k, n, **kw):
                return pe.matmul(o, lhsT, rhs, start=(k == 0), stop=(k == n - 1), **kw)

            def a_transpose(c):
                pe.wait_ge(xn_ready, c + 1)
                pe.wait_ge(xT_copied, 2 * c)
                for k in range(KT):
                    for blk in range(BLK):
                        i = pe.transpose(ps[:, k, blk * P:(blk + 1) * P], xn_a[:, blk, k * P:(k + 1) * P], ident[:])
                    i.then_inc(tr_done, 1)

            def a_v(c, par, half):
                if half == 0:
                    pe.wait_ge(xT_copied, 2 * c + 2)
                pe.wait_ge(v_copied, 2 * c + half)
                for b in range(2):
                    blk = 2 * half + b
                    for k in range(KT):
                        i = mm(ps[:, 2, b * E:(b + 1) * E],
                               xnT_a[:, par, k, blk * P:(blk + 1) * P], w_qkv[:, k, 2 * E:3 * E], k, KT)
                i.then_inc(v_mm_done, 1)

            def a_qk(c, m, par, first):
                if not first:
                    pe.wait_ge(rest_done, 4 * c + m - 3)
                for k in range(KT):
                    i = mm(ps[:, 4 + m, :], w_qkv[:, k, m * P:(m + 1) * P], xnT_a[:, par, k, :], k, KT)
                i.then_inc(qk_mm_done, 1)

            def early_tile(t):
                j, blk, half = t // 8, (t % 8) // 2, t % 2
                if t:
                    pe.wait_ge(max_reduced, t)
                pe.matmul(ps[:, 3, :], Qs[0][0:STACK, j, blk * P:(blk + 1) * P],
                          Ks[0][0:STACK, j, half * 512:(half + 1) * 512], start=True, stop=True).then_inc(max_mm_done, 1)

            def phase_a(c, par, last=False, early=None):
                def tile(k):
                    if early is not None:
                        early_tile(early + k)
                first = isinstance(c, int) and c == 0
                tile(0)
                a_v(c, par, 0)
                tile(1)
                a_qk(c, 0, par, first)
                tile(2)
                a_v(c, par, 1)
                if not last:
                    a_transpose(c + 1)
                for m in range(1, 4):
                    tile(2 + m)
                    a_qk(c, m, par, first)
                tile(6)
                tile(7)

            pe.wait_ge(a_weights, 16 * 4)
            pe.wait_ge(const_set, 4)
            pe.wait_ge(ident_b_set, 1)
            a_transpose(0)
            phase_a(0, 0)
            phase_a(1, 1)
            with pe.Fori(2, EARLY, 2) as c:
                phase_a(c, 0)
                phase_a(c + 1, 1)
            pe.wait_ge(group_loaded[0], GROUP_LOADS)
            for c in range(EARLY, NCH):
                phase_a(c, c % 2, c == NCH - 1, 8 * (c - EARLY))

            def prepare(n):
                if n == 0:
                    pe.wait_ge(c_weights, C_LOADS)
                    pe.wait_ge(max_reduced, MAXT * GROUPS)
                    pe.wait_ge(m_copied, 2 * GROUPS)
                    for m in range(KT):
                        for k in range(KT):
                            i = mm(ps[:, 5, m * B * CTX:(m + 1) * B * CTX].rearrange("p (b t) -> p b t", b=B),
                                   w_k2[:, k, m * P:(m + 1) * P], ctx_dup[:, k, :, 0, :], k, KT)
                elif n <= 2:
                    for b in (2 * n - 2, 2 * n - 1):
                        for k in range(KT):
                            i = mm(ps[:, 5 + n, (b % 2) * E:(b % 2 + 1) * E],
                                   ctx_dup[:, k, b, :, :].rearrange("p c t -> p (c t)"), w_v2[:, k, :], k, KT)
                elif n == 4:
                    pe.wait_ge(prep_done, PREP_STEPS - 1)
                    lb = vx[:, 0:2].rearrange("p b h d -> p (b h d)")
                    for t in range(HT):
                        i = mm(ps[:, 6, 0:E], lb[:, t * P:(t + 1) * P], t_p[:, t, :], t, HT)
                else:
                    pe.wait_ge(abs_summed, 2)
                    pe.wait_ge(prep_done, 1)
                    i = pe.matmul(ps[:, 5, 0:2], ones[:], abs_sum[:], start=True, stop=True)
                i.then_inc(prep_mm, 1)

            pe.wait_ge(rest_done, 4 * NCH)

            def slot_free(G, k, first):
                k -= 3
                if k in M_SLOTS:
                    f = 2 * G + (0 if k == M_SLOTS[0] else -1)
                    if not (first and k == M_SLOTS[1]):
                        pe.wait_ge(m_copied, f + 1)
                elif k >= 0:
                    t = [max_slot(t) for t in range(MAXT)].index(k)
                    pe.wait_ge(max_reduced, MAXT * G + t + 1)
                elif not first:
                    pe.wait_ge(max_reduced, MAXT * G + k + 1)

            def max_tile(G, g, t, first=False):
                qc, i = divmod(t, MAXT // 2)
                j, blk, half = i // 8, (i % 8) // 2, i % 2
                q0 = qc * CH + blk * P
                slot_free(G, max_slot(t), first)
                pe.matmul(ps[:, 5 + max_slot(t) % 3, :], Qs[g][0:STACK, j, q0:q0 + P],
                          Ks[g][0:STACK, j, half * 512:(half + 1) * 512], start=True, stop=True).then_inc(max_mm_done, 1)

            def max_transpose(G, f, qc, last=False):
                k = M_SLOTS[qc]
                if last:
                    pe.wait_ge(max_reduced, MAXT * GROUPS)
                else:
                    slot_free(G, k, False)
                pe.wait_ge(m_split, 2 * f + 2)
                pe.transpose(ps[:, 5 + k % 3, :].bitcast(BF16)[0:96, 0:P], msp[:].rearrange("p s i -> p (s i)"),
                             ident_b[:]).then_inc(m_transposed, 1)

            def scores(U, g, s, h, free=True):
                qc, kb = divmod(s, KB)
                if free:
                    pe.wait_ge(exp_done, 2 * U + h - 1)
                for j in (2 * h, 2 * h + 1):
                    i = pe.matmul(ps[:, j, :], Ks[g][0:ROWS, j, kb * P:(kb + 1) * P],
                                  Qs[g][0:ROWS, j, qc * CH:(qc + 1) * CH], start=True, stop=True)
                i.then_inc(st_done, 1)

            def values(G, g, U, s):
                qc, kb = divmod(s, KB)
                pe.wait_ge(exp_done, 2 * U + 2)
                if kb == 0:
                    pe.wait_ge(o_copied, 2 * G + qc)
                for j in range(HG):
                    i = pe.matmul(ps[32 * j:32 * j + 32, 4, :], Vs[g][:, kb, 32 * j:32 * j + 32],
                                  prob[:, s % 2, j // 2, j % 2, :], start=(kb == 0), stop=(kb == KB - 1))
                i.then_inc(pv_done, 1)

            pe.wait_ge(const_set, 4 + NG)
            for t in range(MAXT // 2, MAXT):
                if t == 40:
                    max_transpose(0, 0, 0)
                max_tile(0, 0, t, True)
            pe.wait_ge(m_loaded, 16)
            scores(0, 0, 0, 0, False)
            scores(0, 0, 0, 1, False)

            def phase_b(b, last):
                for g in range(NG):
                    G = b * NG + g
                    end = last and g == NG - 1
                    g1 = (g + 1) % NG
                    for s in range(UNITS):
                        U = G * UNITS + s
                        if s == 0 and not end:
                            pe.wait_ge(group_loaded[g1], GROUP_LOADS * (b + (g + 1) // NG + 1))
                        if s == 2:
                            max_transpose(G + 1, 2 * G + 1, 1, end)
                        if s == 10 and not end:
                            max_transpose(G + 1, 2 * G + 2, 0)
                        if s == KB - 1:
                            pe.wait_ge(m_loaded, 16 * (2 * G + 2))
                        if s == UNITS - 1 and not end:
                            pe.wait_ge(m_loaded, 16 * (2 * G + 3))
                        for h in range(2):
                            if not end:
                                max_tile(G + 1, g1, 4 * s + h)
                            if not (end and s == UNITS - 1):
                                nxt = (g1, 0) if s == UNITS - 1 else (g, s + 1)
                                scores(U + 1, nxt[0], nxt[1], h)
                        if not end:
                            max_tile(G + 1, g1, 4 * s + 2)
                        values(G, g, U, s)
                        if end and s % 2 == 0 and 4 <= s < 12:
                            prepare(s // 2 - 2)
                        if not end:
                            max_tile(G + 1, g1, 4 * s + 3)

            phase_b(0, False)
            with pe.Fori(1, B - 1) as b:
                phase_b(b, False)
            phase_b(B - 1, True)

            pe.wait_ge(o_copied, 2 * GROUPS)
            pe.wait_ge(max_reduced, MAXT * GROUPS)
            pe.wait_ge(m_copied, 2 * GROUPS)
            prepare(4)

            def x_bank(c, i):
                before = i - 4
                if is_score(before):
                    m = 0 if before < X_S[1] else 1
                    pe.wait_ge(exp2_done, 8 * c + 4 * m + before - X_S[m] + 1)
                else:
                    pe.wait_ge(x_free[i % 4], free_count(c, i))
                return i % 4

            def pair_of_blocks(r, t, lhs, w):
                for h in range(2):
                    blk = 2 * t + h
                    for k in range(KT):
                        n = mm(ps[:, r, h * E:(h + 1) * E], lhs[:, k, blk * P:(blk + 1) * P], w[:, k, :], k, KT)
                n.then_inc(x_done, 1)

            def transposes(c, i, xn):
                for k in range(KT):
                    r = x_bank(c, i + k)
                    for blk in range(BLK):
                        n = pe.transpose(ps[:, r, blk * P:(blk + 1) * P], xn[:, blk, k * P:(k + 1) * P], ident[:])
                    n.then_inc(x_done, 1)

            def ready(c, i):
                pe.wait_ge(x_free[i % 4], free_count(c, i) + 1)

            def q2(c):
                for k in range(KT):
                    ready(c, X_T2 + k)
                for m in range(KT):
                    r = x_bank(c, X_Q2 + m)
                    for k in range(KT):
                        n = mm(ps[:, r, :], w_q2[:, k, m * P:(m + 1) * P], xn2T[:, k, :], k, KT)
                    n.then_inc(x_done, 1)

            def x_scores(c, m, blocks):
                if blocks[0] == 0:
                    if m == 0:
                        pe.wait_ge(kv_copied, 2 * c + 2)
                        ready(c, X_Q2)
                    else:
                        ready(c, X_Q2 + 1)
                for blk in blocks:
                    r = x_bank(c, X_S[m] + blk)
                    pe.matmul(ps[:, r, :], q2T[:, m, blk * P:(blk + 1) * P], kcur[:, m * 8 * CTX:(m + 1) * 8 * CTX],
                              start=True, stop=True).then_inc(x_done, 1)

            def x_pT(c, m, blocks):
                for blk in blocks:
                    r = x_bank(c, X_PT[m] + blk)
                    pe.wait_ge(p_ready, 8 * c + 4 * m + blk + 1)
                    for pr in range(4):
                        n = pe.transpose(ps[:, r, pr * P:(pr + 1) * P], pe_[:, blk, pr * P:(pr + 1) * P], ident[:])
                    n.then_inc(x_done, 1)

            def x_values(c):
                for m in range(KT):
                    for blk in range(BLK):
                        ready(c, X_PT[m] + blk)
                    r = x_bank(c, X_PV + m)
                    for pr in range(4):
                        n = pe.matmul(ps[32 * pr:32 * pr + 32, r, :], vcur[:, 4 * m + pr, :], pT[:, m, pr, :],
                                      start=True, stop=True)
                    n.then_inc(x_done, 1)

            def fc(c, blk, base=4):
                if blk == 0:
                    for i in (X_T3, X_T3 + 1):
                        ready(c, i)
                    if base:
                        pe.wait_ge(ft_ready, HT * c)
                elif blk == 1:
                    if base:
                        pe.wait_ge(out_added, 2 * c)
                else:
                    pe.wait_ge(gelu_done, BLK * c + blk - 1)
                for h in range(2):
                    for n, (part, k) in enumerate((part, k) for part in range(2) for k in range(KT)):
                        i = mm(ps[:, base + 2 * (blk % 2) + h, :], xn3T[:, part, k, blk * P:(blk + 1) * P].bitcast(F32R),
                               t_fc[:, k, h * 512:(h + 1) * 512].bitcast(F32R), n, 2 * KT)
                i.then_inc(fc_done, 1)

            def f_tile(c, t, src=xhat):
                if t < HT:
                    if t == 0:
                        pe.wait_ge(xhat_done, BLK * (c + 1))
                    elif t >= 2:
                        pe.wait_ge(ft_ready, HT * c + t - 1)
                    for blk in range(BLK):
                        i = pe.transpose(ps[:, 4 + t % 2, blk * P:(blk + 1) * P], src[:, blk, t * P:(t + 1) * P], ident[:])
                    i.then_inc(hT_done, 1)
                if t >= 1:
                    pe.wait_ge(ft_ready, HT * c + t)
                    for blk in range(BLK):
                        for part in range(2):
                            i = pe.matmul(ps[:, 6 + blk // 2, (blk % 2) * E:(blk % 2 + 1) * E],
                                          fT[:, (t - 1) % 2, part, blk * P:(blk + 1) * P].bitcast(F32R),
                                          t_p[:, t - 1, :].bitcast(F32R),
                                          start=(t == 1 and blk % 2 == 0 and part == 0), stop=(t == HT and part == 1),
                                          skip_group_check=True)
                    if t == HT:
                        i.then_inc(acc_done, 1)

            def phase_c(c, c_min=2, last=False):
                def second(f, *a):
                    if c_min >= 2:
                        f(c - 2, *a)

                def first(f, *a):
                    if c_min >= 1:
                        f(c - 1, *a)

                second(f_tile, 2)
                pe.wait_ge(xn_ready, NCH + 2 * c + 1)
                transposes(c, X_T2, xn_1)
                second(f_tile, 3)
                q2(c)
                x_scores(c, 0, (0, 1))
                second(f_tile, 4)
                x_scores(c, 0, (2, 3))
                second(f_tile, 5)
                x_pT(c, 0, (0, 1))
                second(f_tile, 6)
                x_pT(c, 0, (2, 3))
                x_scores(c, 1, (0, 1))
                second(f_tile, 7)
                x_scores(c, 1, (2, 3))
                second(f_tile, 8)
                first(fc, 0)
                x_pT(c, 1, (0, 1))
                first(fc, 1)
                x_pT(c, 1, (2, 3))
                x_values(c)
                first(fc, 2)
                first(fc, 3)
                for k in range(KT):
                    ready(c, X_PV + k)
                for t in range(2):
                    pair_of_blocks(x_bank(c, X_O2 + t), t, o2T, w_o2)
                if not last:
                    pe.wait_ge(o_normed, c + 2)
                    for t in range(2):
                        pair_of_blocks(x_bank(c, X_OUT[t]), t, onT, w_out)
                first(f_tile, 0)
                first(f_tile, 1)
                pe.wait_ge(xn_ready, NCH + 2 * c + 2)
                transposes(c, X_T3, xn_2)

            pe.wait_ge(o_normed, 1)
            for t in range(2):
                pair_of_blocks(X_OUT[t] % 4, t, onT, w_out)
            phase_c(0, 0)
            phase_c(1, 1)
            with pe.Fori(2, NCH - 1) as c:
                phase_c(c)
            phase_c(NCH - 1, last=True)
            for blk in range(BLK):
                for t in TAIL[blk]:
                    f_tile(NCH - 2, t)
                fc(NCH - 1, blk, 0)
            f_tile(NCH - 2, HT)
            for t in range(HT + 1):
                f_tile(NCH - 1, t, xhat_last)


def kernel(x, ctx_1024, L0_attn_W_qkv, L0_attn_b_qkv, L0_attn_W_out, L0_attn_b_out,
           L0_xattn_Wq, L0_xattn_bq, L0_xattn_Wk, L0_xattn_bk, L0_xattn_Wv, L0_xattn_bv, L0_xattn_Wo, L0_xattn_bo,
           L0_ffn_W_fc, L0_ffn_ln_w, L0_ffn_ln_b, L0_ffn_W_proj):
    import numpy as np
    import concourse.bacc as bacc
    from concourse.bass_utils import run_bass_kernel_spmd

    def columns(v):
        return np.asarray(v).reshape(-1, P).T

    rows = np.arange(P)[:, None]
    arrays = {
        "x": np.asarray(x).reshape(T, E),
        "ctxT": np.asarray(ctx_1024).reshape(B * CTX, E).T,
        "wqkv": L0_attn_W_qkv, "bqk": columns(np.asarray(L0_attn_b_qkv)[:2 * E]), "bv": np.asarray(L0_attn_b_qkv)[2 * E:],
        "wout": L0_attn_W_out, "bout": L0_attn_b_out,
        "wqT": np.asarray(L0_xattn_Wq).T, "bq2": columns(L0_xattn_bq),
        "wkT": np.asarray(L0_xattn_Wk).T, "bk2": columns(L0_xattn_bk),
        "wvT": np.asarray(L0_xattn_Wv).T, "bv2": L0_xattn_bv,
        "woT": np.asarray(L0_xattn_Wo).T, "bo2": L0_xattn_bo,
        "wfcT": np.asarray(L0_ffn_W_fc).T, "lnw": columns(L0_ffn_ln_w), "lnb": columns(L0_ffn_ln_b),
        "wpT": np.asarray(L0_ffn_W_proj).T,
        "ident": np.eye(P, dtype=np.float32),
        "head_mask": (rows // D == np.arange(8)[None]).astype(np.float32),
        "half_mask": (rows // CTX == np.arange(2)[None]).astype(np.float32),
    }
    arrays = {f"in_{n}": np.ascontiguousarray(a) for n, a in arrays.items()}
    nc = bacc.Bacc("TRN2", target_bir_lowering=False, num_devices=1)
    args = [nc.dram_tensor(n, a.shape, mybir.dt.from_np(a.dtype), kind="ExternalInput").ap() for n, a in arrays.items()]
    out = nc.dram_tensor("out", (T, E), F32, kind="ExternalOutput").ap()
    build(nc, *args, out)
    r = run_bass_kernel_spmd(nc, [arrays], core_ids=[0])
    return r.results[0]["out"].reshape(B, S, E)
```
